# Optimizing a Trainium2 kernel written in Bass

```python
import numpy as np
import jax
import jax.numpy as jnp

def _softmax(x, axis=-1):
    return jax.nn.softmax(x, axis=axis)

def _gelu(x):
    return jax.nn.gelu(x, approximate=True)

def _silu(x):
    return jax.nn.silu(x)

def _sigmoid(x):
    return jax.nn.sigmoid(x)

def _layernorm(x, axis=-1, eps=1e-05):
    m = jnp.mean(x, axis=axis, keepdims=True)
    v = jnp.var(x, axis=axis, keepdims=True)
    return (x - m) / jnp.sqrt(v + eps)

def _scatter_add(tgt, idx, src, axis=0):
    return tgt.at[idx].add(src)

def _segment_sum(src, seg, n):
    return jax.ops.segment_sum(src, seg, n)
kernel_name = 'mk_recurrent_d1_jaxref_r8_177ea9'

def setup_inputs(seed: int=0):
    np.random.seed(seed)
    _w = jnp.asarray

    def _L0_attn_setup():
        import jax, jax.numpy as jnp
        import numpy as np
        B_SZ, T, D_IN, H = (8, 128, 128, 128)
        key = jax.random.key(seed)
        ks = jax.random.split(key, 9)
        lim_u = 1.0 / np.sqrt(D_IN)
        return {'x': jax.random.normal(ks[0], (B_SZ, T, D_IN), dtype=jnp.float32), 'W_u': jax.random.uniform(ks[1], (H, D_IN), jnp.float32, -lim_u, lim_u), 'b_u': jax.random.uniform(ks[2], (H,), jnp.float32, -lim_u, lim_u), 'W_g': jax.random.uniform(ks[3], (H, D_IN), jnp.float32, -lim_u, lim_u), 'b_g': jax.random.uniform(ks[4], (H,), jnp.float32, -lim_u, lim_u), 'A': jnp.eye(H, dtype=jnp.float32) * 0.6, 'Bm': jax.random.normal(ks[5], (H, H), dtype=jnp.float32), 'Cm': jax.random.normal(ks[6], (H, H), dtype=jnp.float32), 'D': jax.random.normal(ks[7], (H,), dtype=jnp.float32)}
    _L0_attn_in = _L0_attn_setup()

    def _L0_ffn_setup():
        import jax, jax.numpy as jnp
        import numpy as np
        DIM = 128
        DEPTH = 6
        HEADS = 16
        DIM_HEAD = 64
        WINDOW = 32
        INNER = HEADS * DIM_HEAD
        DIM_INNER = int(DIM * 4 * 2 / 3)
        QK_SCALE = 8.0

        def shift_tokens(t):
            a, s = jnp.split(t, 2, -1)
            s = jnp.pad(s, ((0, 0), (1, 0), (0, 0)))[:, :-1]
            return jnp.concatenate([a, s], -1)

        def l2norm(t):
            return t / jnp.maximum(jnp.linalg.norm(t, axis=-1, keepdims=True), 1e-12)

        def rotate_half(x):
            x1, x2 = jnp.split(x, 2, -1)
            return jnp.concatenate([-x2, x1], -1)

        def rotary_tables(n):
            half = jnp.arange(0, DIM_HEAD, 2, dtype=jnp.float32)
            inv_freq = 1.0 / 10000.0 ** (half / DIM_HEAD)
            t = jnp.arange(n, dtype=jnp.float32)
            freqs = t[:, None] * inv_freq[None, :]
            freqs = jnp.concatenate([freqs, freqs], -1)
            base_scale = (half + 0.4 * DIM_HEAD) / (1.4 * DIM_HEAD)
            power = (t - n // 2) / (WINDOW // 2)
            scale = base_scale[None, :] ** power[:, None]
            scale = jnp.concatenate([scale, scale], -1)
            return (freqs, scale)

        def local_attention(q, k, v):
            b, h, n, d = q.shape
            w = WINDOW
            nw = n // w
            bq = q.reshape(b, h, nw, w, d)
            bk = k.reshape(b, h, nw, w, d)
            bv = v.reshape(b, h, nw, w, d)

            def look(t):
                p = jnp.pad(t, ((0, 0), (0, 0), (1, 0), (0, 0), (0, 0)))
                return jnp.concatenate([p[:, :, :nw], p[:, :, 1:]], axis=3)
            bk2, bv2 = (look(bk), look(bv))
            seq = jnp.arange(n).reshape(nw, w)
            seq_p = jnp.pad(seq, ((1, 0), (0, 0)), constant_values=-1)
            jt = jnp.concatenate([seq_p[:nw], seq_p[1:]], axis=1)
            it = seq[:, :, None]
            jb = jt[:, None, :]
            mask = (it < jb) | (it > jb + w) | (jb == -1)
            sim = jnp.einsum('bhwie,bhwje->bhwij', bq, bk2) * QK_SCALE
            sim = jnp.where(mask, -jnp.finfo(sim.dtype).max, sim)
            attn = jax.nn.softmax(sim, -1)
            out = jnp.einsum('bhwij,bhwje->bhwie', attn, bv2)
            return out.reshape(b, h, n, d)

        def attn_layer(x, Wqkv, qs, ksc, Wo):
            b, n, _ = x.shape
            qkv = x @ Wqkv
            q, k, v = jnp.split(qkv, 3, -1)
            sh = lambda t: t.reshape(b, n, HEADS, DIM_HEAD).transpose(0, 2, 1, 3)
            q, k, v = (sh(q), sh(k), sh(v))
            q = l2norm(q) * qs
            k = l2norm(k) * ksc
            freqs, scale = rotary_tables(n)
            cos, sin = (jnp.cos(freqs), jnp.sin(freqs))
            q = q * cos * scale + rotate_half(q) * sin * scale
            inv = 1.0 / scale
            k = k * cos * inv + rotate_half(k) * sin * inv
            out = local_attention(q, k, v)
            out = out.transpose(0, 2, 1, 3).reshape(b, n, INNER)
            return out @ Wo

        def ffn_layer(x, g, bln, W1, b1, W2, b2):
            mu = x.mean(-1, keepdims=True)
            var = ((x - mu) ** 2).mean(-1, keepdims=True)
            xn = (x - mu) / jnp.sqrt(var + 1e-05) * g + bln
            hg = xn @ W1 + b1
            a, gate = jnp.split(hg, 2, -1)
            return a * jax.nn.gelu(gate, approximate=False) @ W2 + b2
        key = jax.random.key(seed)
        ks = jax.random.split(key, 8)
        B, N = (2, 256)
        init = lambda k, shape: jax.random.normal(k, shape, jnp.float32) * 0.02
        return {'x': jax.random.normal(ks[0], (B, N, DIM), jnp.float32), 'Wqkv': init(ks[1], (DEPTH, DIM, 3 * INNER)), 'q_scale': jnp.ones((DEPTH, DIM_HEAD), jnp.float32), 'k_scale': jnp.ones((DEPTH, DIM_HEAD), jnp.float32), 'Wo': init(ks[2], (DEPTH, INNER, DIM)), 'ln_g': jnp.ones((DEPTH, DIM), jnp.float32), 'ln_b': jnp.zeros((DEPTH, DIM), jnp.float32), 'W1': init(ks[3], (DEPTH, DIM, 2 * DIM_INNER)), 'b1': jnp.zeros((DEPTH, 2 * DIM_INNER), jnp.float32), 'W2': init(ks[4], (DEPTH, DIM_INNER, DIM)), 'b2': jnp.zeros((DEPTH, DIM), jnp.float32)}
    _L0_ffn_in = _L0_ffn_setup()
    _d = {'L0_attn_x': _L0_attn_in['x'], 'L0_attn_W_u': _L0_attn_in['W_u'], 'L0_attn_b_u': _L0_attn_in['b_u'], 'L0_attn_W_g': _L0_attn_in['W_g'], 'L0_attn_b_g': _L0_attn_in['b_g'], 'L0_attn_A': _L0_attn_in['A'], 'L0_attn_Bm': _L0_attn_in['Bm'], 'L0_attn_Cm': _L0_attn_in['Cm'], 'L0_attn_D': _L0_attn_in['D'], 'L0_ffn_Wqkv': _L0_ffn_in['Wqkv'], 'L0_ffn_q_scale': _L0_ffn_in['q_scale'], 'L0_ffn_k_scale': _L0_ffn_in['k_scale'], 'L0_ffn_Wo': _L0_ffn_in['Wo'], 'L0_ffn_ln_g': _L0_ffn_in['ln_g'], 'L0_ffn_ln_b': _L0_ffn_in['ln_b'], 'L0_ffn_W1': _L0_ffn_in['W1'], 'L0_ffn_b1': _L0_ffn_in['b1'], 'L0_ffn_W2': _L0_ffn_in['W2'], 'L0_ffn_b2': _L0_ffn_in['b2']}
    _x0 = _d['L0_attn_x']
    _d['L0_attn_x'] = jax.random.normal(jax.random.fold_in(jax.random.key(seed), 1), (8, 256, 128), dtype=_x0.dtype)
    del _x0
    return _d

def reference(L0_attn_x, L0_attn_W_u, L0_attn_b_u, L0_attn_W_g, L0_attn_b_g, L0_attn_A, L0_attn_Bm, L0_attn_Cm, L0_attn_D, L0_ffn_Wqkv, L0_ffn_q_scale, L0_ffn_k_scale, L0_ffn_Wo, L0_ffn_ln_g, L0_ffn_ln_b, L0_ffn_W1, L0_ffn_b1, L0_ffn_W2, L0_ffn_b2):

    def _L0_attn_ref(x, W_u, b_u, W_g, b_g, A, Bm, Cm, D):
        import jax, jax.numpy as jnp
        import numpy as np
        B_SZ, T, D_IN, H = (8, 128, 128, 128)
        u = jax.nn.gelu(jnp.einsum('btd,hd->bth', x, W_u) + b_u, approximate=False) * jax.nn.sigmoid(jnp.einsum('btd,hd->bth', x, W_g) + b_g)
        uB = jnp.einsum('btd,hd->tbh', u, Bm)

        def step(s, uB_t):
            s = s @ A.T + uB_t
            y = s @ Cm.T + D
            return (s, y)
        s0 = jnp.zeros((x.shape[0], A.shape[0]), dtype=x.dtype)
        _, ys = jax.lax.scan(step, s0, uB)
        return jnp.transpose(ys, (1, 0, 2))

    def _L0_ffn_ref(x, Wqkv, q_scale, k_scale, Wo, ln_g, ln_b, W1, b1, W2, b2):
        import jax, jax.numpy as jnp
        import numpy as np
        DIM = 128
        DEPTH = 6
        HEADS = 16
        DIM_HEAD = 64
        WINDOW = 32
        INNER = HEADS * DIM_HEAD
        DIM_INNER = int(DIM * 4 * 2 / 3)
        QK_SCALE = 8.0

        def shift_tokens(t):
            a, s = jnp.split(t, 2, -1)
            s = jnp.pad(s, ((0, 0), (1, 0), (0, 0)))[:, :-1]
            return jnp.concatenate([a, s], -1)

        def l2norm(t):
            return t / jnp.maximum(jnp.linalg.norm(t, axis=-1, keepdims=True), 1e-12)

        def rotate_half(x):
            x1, x2 = jnp.split(x, 2, -1)
            return jnp.concatenate([-x2, x1], -1)

        def rotary_tables(n):
            half = jnp.arange(0, DIM_HEAD, 2, dtype=jnp.float32)
            inv_freq = 1.0 / 10000.0 ** (half / DIM_HEAD)
            t = jnp.arange(n, dtype=jnp.float32)
            freqs = t[:, None] * inv_freq[None, :]
            freqs = jnp.concatenate([freqs, freqs], -1)
            base_scale = (half + 0.4 * DIM_HEAD) / (1.4 * DIM_HEAD)
            power = (t - n // 2) / (WINDOW // 2)
            scale = base_scale[None, :] ** power[:, None]
            scale = jnp.concatenate([scale, scale], -1)
            return (freqs, scale)

        def local_attention(q, k, v):
            b, h, n, d = q.shape
            w = WINDOW
            nw = n // w
            bq = q.reshape(b, h, nw, w, d)
            bk = k.reshape(b, h, nw, w, d)
            bv = v.reshape(b, h, nw, w, d)

            def look(t):
                p = jnp.pad(t, ((0, 0), (0, 0), (1, 0), (0, 0), (0, 0)))
                return jnp.concatenate([p[:, :, :nw], p[:, :, 1:]], axis=3)
            bk2, bv2 = (look(bk), look(bv))
            seq = jnp.arange(n).reshape(nw, w)
            seq_p = jnp.pad(seq, ((1, 0), (0, 0)), constant_values=-1)
            jt = jnp.concatenate([seq_p[:nw], seq_p[1:]], axis=1)
            it = seq[:, :, None]
            jb = jt[:, None, :]
            mask = (it < jb) | (it > jb + w) | (jb == -1)
            sim = jnp.einsum('bhwie,bhwje->bhwij', bq, bk2) * QK_SCALE
            sim = jnp.where(mask, -jnp.finfo(sim.dtype).max, sim)
            attn = jax.nn.softmax(sim, -1)
            out = jnp.einsum('bhwij,bhwje->bhwie', attn, bv2)
            return out.reshape(b, h, n, d)

        def attn_layer(x, Wqkv, qs, ksc, Wo):
            b, n, _ = x.shape
            qkv = x @ Wqkv
            q, k, v = jnp.split(qkv, 3, -1)
            sh = lambda t: t.reshape(b, n, HEADS, DIM_HEAD).transpose(0, 2, 1, 3)
            q, k, v = (sh(q), sh(k), sh(v))
            q = l2norm(q) * qs
            k = l2norm(k) * ksc
            freqs, scale = rotary_tables(n)
            cos, sin = (jnp.cos(freqs), jnp.sin(freqs))
            q = q * cos * scale + rotate_half(q) * sin * scale
            inv = 1.0 / scale
            k = k * cos * inv + rotate_half(k) * sin * inv
            out = local_attention(q, k, v)
            out = out.transpose(0, 2, 1, 3).reshape(b, n, INNER)
            return out @ Wo

        def ffn_layer(x, g, bln, W1, b1, W2, b2):
            mu = x.mean(-1, keepdims=True)
            var = ((x - mu) ** 2).mean(-1, keepdims=True)
            xn = (x - mu) / jnp.sqrt(var + 1e-05) * g + bln
            hg = xn @ W1 + b1
            a, gate = jnp.split(hg, 2, -1)
            return a * jax.nn.gelu(gate, approximate=False) @ W2 + b2
        for i in range(DEPTH):
            x = attn_layer(shift_tokens(x), Wqkv[i], q_scale[i], k_scale[i], Wo[i]) + x
            x = ffn_layer(shift_tokens(x), ln_g[i], ln_b[i], W1[i], b1[i], W2[i], b2[i]) + x
        return x
    x = L0_attn_x
    xn = _layernorm(x, axis=-1)
    s = _L0_attn_ref(xn, L0_attn_W_u, L0_attn_b_u, L0_attn_W_g, L0_attn_b_g, L0_attn_A, L0_attn_Bm, L0_attn_Cm, L0_attn_D)
    g = _silu(_L0_ffn_ref(xn, L0_ffn_Wqkv, L0_ffn_q_scale, L0_ffn_k_scale, L0_ffn_Wo, L0_ffn_ln_g, L0_ffn_ln_b, L0_ffn_W1, L0_ffn_b1, L0_ffn_W2, L0_ffn_b2))
    x = x + s * g
    return x

_drawn_inputs = setup_inputs


def setup_inputs(seed=0):
    import zlib

    import numpy as np

    out = dict(_drawn_inputs(seed))
    spreads = {'L0_ffn_q_scale': (1.0, 0.6),
     'L0_ffn_k_scale': (1.0, 0.6),
     'L0_ffn_ln_g': (1.0, 0.6),
     'L0_ffn_ln_b': (0.0, 0.8),
     'L0_ffn_b1': (0.0, 0.472),
     'L0_ffn_b2': (0.0, 0.1)}
    factors = {}
    for name, (base, spread) in spreads.items():
        noise = np.random.default_rng([zlib.crc32(name.encode()), seed]).standard_normal(out[name].shape)
        drawn = base * np.exp(spread * noise) if base else spread * noise
        out[name] = jnp.asarray(drawn.astype(out[name].dtype))
    for name, factor in factors.items():
        out[name] = (out[name] * factor).astype(out[name].dtype)
    return out
```

```python
from contextlib import ExitStack

import numpy as np

import concourse.bass as bass
from concourse import mybir

F32 = mybir.dt.float32
BF16 = mybir.dt.bfloat16
I32 = mybir.dt.int32
ALU = mybir.AluOpType
ACT = mybir.ActivationFunctionType
AX_X = mybir.AxisListType.X

P = 128
B, N, D = 8, 256, 128
DEPTH, HEADS, DH, WINDOW = 6, 16, 64, 32
INNER = HEADS * DH
FF = int(D * 4 * 2 / 3)
FCH = [(c * P, min(P, FF - c * P)) for c in range(-(-FF // P))]
NCH = len(FCH)
QK_SCALE = 8.0
STEPS = DEPTH * B
SLOTS = 8
UNITS = STEPS * SLOTS
LAG = 3
HP = HEADS // 2
QB = N // 64
KW = 96
PAD = WINDOW
NT = N // P
T = B * N
TILES = T // P
RSQRT_SEED = 1597463007.0 - 2 ** 22
NEWTON = 3
C_ID, C_MASK, C_TAB = 0, P, P + QB * KW
C_ALL = C_TAB + 4 * NT * DH
R_G, R_B, R_B1A, R_B1G, R_B2 = 0, 1, 2, 2 + NCH, 2 + 2 * NCH
R_ALL = 3 + 2 * NCH


def live(unit, count):
    return 0 <= unit < count if isinstance(unit, int) else True


def wait(eng, sem, count):
    if not isinstance(count, int) or count > 0:
        eng.wait_ge(sem, count)


def all_steps(eng, step):
    for s in range(4):
        step(s, s % 2)
    with eng.Fori(2, STEPS // 2) as j:
        step(2 * j, 0)
        step(2 * j + 1, 1)
    step(STEPS, 0)
    step(STEPS + 1, 1)


def gated_mix_kernel(nc, x, rec_w, rec_b, wqkv, wo, w1, w2, params, qk_scales, consts, out):
    with ExitStack() as ctx:
        def sb(name, shape, dt=F32):
            return ctx.enter_context(nc.sbuf_tensor(name, shape, dt))

        def sem(name):
            return ctx.enter_context(nc.semaphore(name))

        cst = sb("cst", [P, C_ALL])
        ident = cst[:, C_ID:C_ID + P]
        ident_bf = sb("ident_bf", [P, P], BF16)
        mask_bf = sb("mask_bf", [P, QB * KW], BF16)
        mean_w = sb("mean_w", [P, P])
        scales = sb("scales", [P, 4, DEPTH, DH])
        wqkv_sb = sb("wqkv_sb", [P, 3 * INNER])
        wo_sb = sb("wo_sb", [P, HP, D])
        w1_sb = sb("w1_sb", [P, 2 * FF])
        w2_sb = sb("w2_sb", [P, NCH, D])
        prm = sb("prm", [P, R_ALL])
        xT = sb("xT", [P, B, N])
        yT = sb("yT", [P, B, N])
        xw = sb("xw", [P, 2, PAD + N])
        table = sb("table", [P, 2, 2, NT, DH])
        sq = sb("sq", [P, 2, 512])
        t1 = sb("t1", [P, 4, 512])
        t2 = sb("t2", [P, 2, 512])
        ss = sb("ss", [P, 2, 16])
        rn = sb("rn", [P, 2, 16])
        hss = sb("hss", [P, 2, 16])
        nwt = sb("nwt", [P, 16])
        c15 = sb("c15", [P, 16])
        QT = sb("QT", [P, 2, HP, QB, 2, 64])
        KT = sb("KT", [P, 2, HP, PAD + N])
        V = sb("V", [P, 2, QB, INNER])
        mx = sb("mx", [P, 2, QB])
        sm = sb("sm", [P, 4, QB])
        rs = sb("rs", [P, 4, QB])
        E = sb("E", [P, 4, QB, KW])
        PT = sb("PT", [KW, 2, QB, P])
        OT = sb("OT", [P, 2, HP, N])
        xm = sb("xm", [P, 2, N])
        xs = sb("xs", [P, N])
        xc = sb("xc", [P, N])
        xq = sb("xq", [P, N])
        std = sb("std", [P, N])
        rstd = sb("rstd", [P, N])
        xr = sb("xr", [P, N])
        xn = sb("xn", [P, N])
        gel = sb("gel", [P, NCH, N])
        hid = sb("hid", [P, NCH, N])
        x_tok = V[:, 0, 0:2, :].rearrange("p a b -> p (a b)").rearrange("p (t d) -> p t d", d=D)
        o_tok = V[:, 0, 2:4, :].rearrange("p a b -> p (a b)").rearrange("p (t d) -> p t d", d=D)
        U = V[:, 1, 0:2, :].rearrange("p a b -> p (a b)")
        G = V[:, 1, 2:4, :].rearrange("p a b -> p (a b)")
        Z = U.rearrange("p (b n) -> p b n", b=B)
        rw = sb("rw", [P, 6, P])
        rb = sb("rb", [P, 3])
        powA = sb("powA", [P, 2, 2, P])
        stats = sb("stats", [P, TILES, 6])
        mv = sb("mv", [P, TILES, 2])
        rst = sb("rst", [P, TILES])
        eps = sb("eps", [P, 1])

        def bank(name):
            return ctx.enter_context(nc.psum_tensor(name, [P, 512], F32))

        S_ps = [bank("S0"), bank("S1")]
        PT_ps = bank("PTb")
        O_ps = bank("Ob")
        F_ps = [bank("F0"), bank("F1")]
        QK_ps = bank("QKb")
        VT_ps = bank("VTb")
        banks = [S_ps[0], S_ps[1], PT_ps, O_ps, F_ps[0], F_ps[1], QK_ps, VT_ps]

        in_x, in_rec, in_cst, in_scl = sem("in_x"), sem("in_rec"), sem("in_cst"), sem("in_scl")
        in_wqk, in_wv, in_wo, in_ffn = sem("in_wqk"), sem("in_wv"), sem("in_wo"), sem("in_ffn")
        set_pool, set_dve = sem("set_pool"), sem("set_dve")
        st_done, mv_done, sd_done, ln_done, lnT_ready, xT_done = (
            sem("st_done"), sem("mv_done"), sem("sd_done"), sem("ln_done"), sem("lnT_ready"), sem("xT_done"))
        rec_mm, rec_act, u_done, uB_ready, Z_done, pow_ready, pow_done, yT_done = (
            sem("rec_mm"), sem("rec_act"), sem("u_done"), sem("uB_ready"), sem("Z_done"), sem("pow_ready"),
            sem("pow_done"), sem("yT_done"))
        scan_ready = sem("scan_ready")
        x_staged, tab_done = sem("x_staged"), sem("tab_done")
        qk_ready, sq_done, t12_done, ss_done = sem("qk_ready"), sem("sq_done"), sem("t12_done"), sem("ss_done")
        seed_done = sem("seed_done")
        add_done, nw_seq, qk_norm = sem("add_done"), sem("nw_seq"), sem("qk_norm")
        tr_ready, tr_evac, v_ready, v_evac = sem("tr_ready"), sem("tr_evac"), sem("v_ready"), sem("v_evac")
        s_ready, max_done, sub_done, exp_done = sem("s_ready"), sem("max_done"), sem("sub_done"), sem("exp_done")
        sum_done, rs_done, p_norm = sem("sum_done"), sem("rs_done"), sem("p_norm")
        pt_ready, pt_evac, o_ready, o_evac = sem("pt_ready"), sem("pt_evac"), sem("o_ready"), sem("o_evac")
        ff_ready, mid_done, xs_done, cent_done, xq_done = (
            sem("ff_ready"), sem("mid_done"), sem("xs_done"), sem("cent_done"), sem("xq_done"))
        std_done, rstd_done, xr_done, xn_done, gel_done, hid_done, ff_final = (
            sem("std_done"), sem("rstd_done"), sem("xr_done"), sem("xn_done"), sem("gel_done"), sem("hid_done"),
            sem("ff_final"))
        g_done, prod_done, oT_ready, o_done, stored = (
            sem("g_done"), sem("prod_done"), sem("oT_ready"), sem("o_done"), sem("stored"))
        in_x2 = sem("in_x2")

        FF_USES = 4 + NCH
        K_WO, K_MEAN, K_VAR, K_W1, K_W2 = 0, 1, 2, 3, 3 + NCH
        NW_OPS = 4 * NEWTON

        block = ctx.enter_context(nc.Block())

        @block.sync
        def _(sp):
            sp.dma_start(x_tok, x.rearrange("b (t p) d -> p (b t) d", p=P)).then_inc(in_x, 16)
            sp.dma_start(cst[:, :], consts).then_inc(in_cst, 16)
            sp.dma_start(rw[:, :, :], rec_w).then_inc(in_rec, 16)
            sp.dma_start(rb[:, :], rec_b).then_inc(in_rec, 16)
            sp.dma_start(wqkv_sb[:, 0:2 * INNER], wqkv[0, :, 0:2 * INNER]).then_inc(in_wqk, 16)
            sp.dma_start(wqkv_sb[:, 2 * INNER:], wqkv[0, :, 2 * INNER:]).then_inc(in_wv, 16)
            sp.dma_start(scales[:, :, :, :], qk_scales).then_inc(in_scl, 16)
            sp.dma_start(wo_sb[:, :, :], wo[0]).then_inc(in_wo, 16)
            sp.dma_start(w1_sb[:, :], w1[0]).then_inc(in_ffn, 16)
            sp.dma_start(w2_sb[:, :, :], w2[0]).then_inc(in_ffn, 16)
            sp.dma_start(prm[:, :], params[0]).then_inc(in_ffn, 16)
            with sp.Fori(1, DEPTH) as l:
                w_l = wqkv[bass.ds(l, 1)].rearrange("o p n -> (o p) n")
                sp.wait_ge(qk_ready, l * (B * SLOTS))
                sp.dma_start(wqkv_sb[:, 0:2 * INNER], w_l[:, 0:2 * INNER]).then_inc(in_wqk, 16)
                sp.wait_ge(v_ready, l * (B * SLOTS))
                sp.dma_start(wqkv_sb[:, 2 * INNER:], w_l[:, 2 * INNER:]).then_inc(in_wv, 16)
                sp.wait_ge(ff_ready, l * (B * FF_USES) - (FF_USES - 1))
                sp.dma_start(wo_sb[:, :, :], wo[bass.ds(l, 1)].rearrange("o p h n -> (o p) h n")).then_inc(in_wo, 16)
                sp.wait_ge(ff_final, l * B)
                sp.dma_start(w1_sb[:, :], w1[bass.ds(l, 1)].rearrange("o p n -> (o p) n")).then_inc(in_ffn, 16)
                sp.dma_start(w2_sb[:, :, :], w2[bass.ds(l, 1)].rearrange("o p c n -> (o p) c n")).then_inc(in_ffn, 16)
                sp.dma_start(prm[:, :], params[bass.ds(l, 1)].rearrange("o p n -> (o p) n")).then_inc(in_ffn, 16)
            sp.wait_ge(o_ready, UNITS)
            sp.dma_start(x_tok, x.rearrange("b (t p) d -> p (b t) d", p=P)).then_inc(in_x2, 16)
            for c in range(4):
                sp.wait_ge(o_done, c + 1)
                sp.dma_start(out[2 * c:2 * c + 2].rearrange("b (t p) d -> p (b t) d", p=P),
                             o_tok[:, 4 * c:4 * c + 4, :]).then_inc(stored, 16)
            sp.wait_ge(stored, 64)

        @block.tensor
        def _(pe):
            pe.wait_ge(in_cst, 16)
            pe.wait_ge(in_rec, 32)
            for t in range(TILES):
                pe.wait_ge(ln_done, t + 1)
                mm = pe.transpose(banks[t // 4][:, (t % 4) * P:(t % 4 + 1) * P], x_tok[:, t, :], ident)
                if t % 4 == 3:
                    mm.then_inc(lnT_ready, 1)
            xf = xT[:, :, :].rearrange("p b n -> p (b n)")
            Zf = U
            for c in range(4):
                pe.wait_ge(xT_done, c + 1)
                for k in range(2):
                    pe.matmul(banks[4 * k + c][:, :], rw[:, k, :], xf[:, 512 * c:512 * (c + 1)],
                              start=True, stop=True).then_inc(rec_mm, 1)
            for c in range(4):
                pe.wait_ge(u_done, c + 1)
                pe.matmul(banks[c][:, :], rw[:, 4, :], G[:, 512 * c:512 * (c + 1)],
                          start=True, stop=True).then_inc(uB_ready, 1)
            k, r = 1, 0
            while k < N:
                at, a_ = (rw[:, 3, :], rw[:, 2, :]) if r == 0 else (powA[:, r % 2, 0, :], powA[:, r % 2, 1, :])
                if r:
                    pe.wait_ge(pow_done, r)
                for c in range(4):
                    pe.wait_ge(Z_done, 4 * r + c + 1)
                    pe.matmul(banks[c][:, 0:2 * (N - k)].rearrange("p (b n) -> p b n", b=2), at,
                              Z[:, 2 * c:2 * c + 2, 0:N - k], start=True, stop=True).then_inc(scan_ready, 1)
                if 2 * k < N:
                    pe.matmul(banks[4 + r % 2][:, 0:P], a_, at, start=True, stop=True)
                    pe.matmul(banks[4 + r % 2][:, P:2 * P], at, a_, start=True, stop=True).then_inc(pow_ready, 1)
                k, r = 2 * k, r + 1
            for c in range(4):
                pe.wait_ge(Z_done, 4 * r + c + 1)
                pe.matmul(banks[4 + c][:, :], rw[:, 5, :], Zf[:, 512 * c:512 * (c + 1)],
                          start=True, stop=True).then_inc(scan_ready, 1)
            pe.wait_ge(yT_done, 4)
            pe.wait_ge(set_pool, 6)
            pe.wait_ge(set_dve, 4)

            def ff_use(s_par_of_f, use):
                return F_ps[(s_par_of_f + use) % 2]

            def step(s, par):
                for v in range(SLOTS):
                    g = s * SLOTS + v
                    a = g - SLOTS
                    if live(g, UNITS):
                        if v == 0:
                            if par == 0:
                                wait(pe, in_wqk, (s // B + 1) * 16)
                            wait(pe, x_staged, 2 * (s + 1))
                        wait(pe, t12_done, 2 * g)
                        half, tile, kind = v // 4, (v // 2) % 2, v % 2
                        pe.matmul(QK_ps[:, :], xw[:, par, PAD + P * tile:PAD + P * (tile + 1)],
                                  wqkv_sb[:, kind * INNER + 512 * half:kind * INNER + 512 * (half + 1)],
                                  start=True, stop=True).then_inc(qk_ready, 1)
                    if live(a, UNITS):
                        if v % 4 == 0:
                            wait(pe, tr_evac, 2 * (a - v + 4 * (v // 4 + 1)))
                        wait(pe, sub_done, a - 1)
                        sp_ = S_ps[v % 2]
                        for m in range(QB):
                            pe.matmul(sp_[:, KW * m:KW * (m + 1)],
                                      QT[:, 1 - par, v, m, :, :].rearrange("p h q -> p (h q)"),
                                      KT[:, 1 - par, v, 64 * m:64 * m + KW],
                                      start=(m == 0), stop=False, skip_group_check=True)
                        mm = pe.matmul(sp_[:, 0:QB * KW], ident_bf[:, :], mask_bf[:, :], start=False, stop=True,
                                       skip_group_check=True)
                        mm.then_inc(s_ready, 1)
                    vu = g - LAG
                    vv = (v - LAG) % SLOTS
                    vpar = par if v >= LAG else 1 - par
                    if live(vu, UNITS):
                        if v == LAG and par == 0:
                            wait(pe, in_wv, (s // B + 1) * 16)
                        wait(pe, v_evac, vu)
                        wait(pe, tr_evac, 2 * vu)
                        m, half = vv // 2, vv % 2
                        pe.matmul(VT_ps[0:KW, :], xw[:, vpar, 64 * m:64 * m + KW],
                                  wqkv_sb[:, 2 * INNER + 512 * half:2 * INNER + 512 * (half + 1)],
                                  start=True, stop=True).then_inc(v_ready, 1)
                    if v == 7 and live(s - 2, STEPS):
                        ff_w1(s - 2, par, [2])
                    a2 = a - 2
                    if live(a2, UNITS):
                        wait(pe, p_norm, a2 + 1)
                        wait(pe, pt_evac, a2)
                        for m in range(QB):
                            mm = pe.transpose(PT_ps[0:KW, P * m:P * (m + 1)], E[:, (v - 2) % 4, m, :], ident)
                        mm.then_inc(pt_ready, 1)
                    a3 = a - 3
                    hp3 = (v - 3) % SLOTS
                    par3 = 1 - par if v >= 3 else par
                    if live(a3, UNITS):
                        if v == 3:
                            wait(pe, v_evac, (s - 1) * SLOTS + SLOTS)
                        wait(pe, pt_evac, a3 + 1)
                        wait(pe, o_evac, a3)
                        for m in range(QB):
                            for h in range(2):
                                mm = pe.matmul(O_ps[64 * h:64 * h + 64, 64 * m:64 * m + 64],
                                               V[0:KW, par3, m, (2 * hp3 + h) * DH:(2 * hp3 + h + 1) * DH],
                                               PT[:, (v - 3) % 2, m, 64 * h:64 * h + 64], start=True, stop=True)
                        mm.then_inc(o_ready, 1)
                    if live(vu, UNITS):
                        wait(pe, qk_norm, vu + 1)
                        wait(pe, v_evac, vu + 1)
                        for i in range(4):
                            mm = pe.transpose(VT_ps[:, P * i:P * (i + 1)], t1[:, (v - LAG) % 4, P * i:P * (i + 1)],
                                              ident)
                        mm.then_inc(tr_ready, 1)
                    f = s - 2
                    if live(f, STEPS):
                        if v == 3:
                            if par == 0:
                                wait(pe, in_wo, (f // B + 1) * 16)
                            wait(pe, o_evac, (f + 1) * SLOTS)
                            for h in range(HP):
                                mm = pe.matmul(ff_use(par, K_WO)[:, 0:N], wo_sb[:, h, :], OT[:, par, h, :],
                                               start=(h == 0), stop=(h == HP - 1))
                            mm.then_inc(ff_ready, 1)
                        if v == 4:
                            wait(pe, xs_done, 2 * (f + 1))
                            pe.matmul(ff_use(par, K_MEAN)[:, 0:N], mean_w[:, :], xs[:, :],
                                      start=True, stop=True).then_inc(ff_ready, 1)
                        if v == 5:
                            wait(pe, xq_done, f + 1)
                            wait(pe, mid_done, f + 1)
                            pe.matmul(ff_use(par, K_VAR)[:, 0:N], mean_w[:, :], xq[:, :],
                                      start=True, stop=True).then_inc(ff_ready, 1)
                        if v == 6:
                            if par == 0:
                                wait(pe, in_ffn, (f // B + 1) * 48)
                            wait(pe, xn_done, f + 1)
                            ff_w1(f, par, [0, 1])
                    f3 = s - 3
                    if v == 1 and live(f3, STEPS):
                        wait(pe, hid_done, (f3 + 1) * NCH)
                        for r_ in range(NCH):
                            mm = pe.matmul(ff_use(1 - par, K_W2)[:, 0:N], w2_sb[:, r_, :], hid[:, r_, :],
                                           start=(r_ == 0), stop=(r_ == NCH - 1))
                        mm.then_inc(ff_ready, 1)

            def ff_w1(f, par, chunks):
                for r_ in chunks:
                    c0, w = FCH[r_]
                    fb = ff_use(par, K_W1 + r_)
                    if r_ == 0:
                        wait(pe, cent_done, f + 1)
                    if r_ == 1:
                        wait(pe, std_done, f + 1)
                    if r_ == 2:
                        wait(pe, hid_done, f * NCH + 1)
                    pe.matmul(fb[0:w, 0:N], w1_sb[:, c0:c0 + w], xn[:, :], start=True, stop=True)
                    pe.matmul(fb[0:w, N:2 * N], w1_sb[:, FF + c0:FF + c0 + w], xn[:, :],
                              start=True, stop=True).then_inc(ff_ready, 1)

            all_steps(pe, step)
            pe.wait_ge(hid_done, STEPS * NCH)
            for r_ in range(NCH):
                mm = pe.matmul(ff_use((STEPS - 1) % 2, K_W2)[:, 0:N], w2_sb[:, r_, :], hid[:, r_, :],
                               start=(r_ == 0), stop=(r_ == NCH - 1))
            mm.then_inc(ff_ready, 1)
            for c in range(4):
                pe.wait_ge(prod_done, c + 1)
                for i in range(4):
                    mm = pe.transpose(banks[c][:, P * i:P * (i + 1)], yT[:, 2 * c + i // 2, (i % 2) * P:(i % 2 + 1) * P],
                                      ident)
                mm.then_inc(oT_ready, 1)

        @block.scalar
        def _(act):
            act.wait_ge(set_dve, 4)
            act.wait_ge(mv_done, TILES)
            act.activation(rst[:, :], mv[:, :, 1], ACT.Sqrt, bias=eps[:, 0:1]).then_inc(sd_done, 1)
            xf = xT[:, :, :].rearrange("p b n -> p (b n)")
            for c in range(4):
                act.wait_ge(lnT_ready, c + 1)
                act.copy(xf[:, 512 * c:512 * (c + 1)], banks[c][:, :]).then_inc(xT_done, 1)
            act.wait_ge(in_rec, 32)
            for c in range(4):
                act.wait_ge(rec_mm, 2 * c + 1)
                act.activation(U[:, 512 * c:512 * (c + 1)], banks[c][:, :], ACT.Gelu,
                               bias=rb[:, 0:1]).then_inc(rec_act, 1)
            for c in range(4):
                act.wait_ge(rec_mm, 2 * c + 2)
                act.activation(G[:, 512 * c:512 * (c + 1)], banks[4 + c][:, :], ACT.Sigmoid,
                               bias=rb[:, 1:2]).then_inc(rec_act, 1)

            def stage(s, par):
                b = s % B
                src = xT[:, b, :] if isinstance(s, int) else xT[:, bass.ds(b, 1), :].rearrange("p o n -> p (o n)")
                act.copy(xw[0:64, par, PAD:PAD + N], src[0:64, :]).then_inc(x_staged, 1)
                act.copy(xw[64:P, par, PAD + 1:PAD + N], src[64:P, 0:N - 1]).then_inc(x_staged, 1)

            act.wait_ge(xT_done, 4)
            act.wait_ge(yT_done, 4)
            act.wait_ge(set_pool, 6)
            stage(0, 0)

            def step(s, par):
                for v in range(SLOTS):
                    g = s * SLOTS + v
                    a = g - SLOTS
                    f = s - 2
                    if v == 6 and live(f, STEPS):
                        wait(act, ff_ready, f * FF_USES + K_VAR + 1)
                        act.activation(std[:, :], F_ps[(par + K_VAR) % 2][:, 0:N], ACT.Sqrt,
                                       bias=eps[:, 0:1]).then_inc(std_done, 1)
                    if v == 7 and live(f, STEPS):
                        gelus(f, par, [0, 1])
                    if live(g, UNITS):
                        wait(act, qk_ready, g + 1)
                        wait(act, ss_done, g - 1)
                        act.activation(sq[:, v % 2, :], QK_ps[:, :], ACT.Square).then_inc(sq_done, 1)
                    vu = g - LAG
                    vv = (v - LAG) % SLOTS
                    vpar = par if v >= LAG else 1 - par
                    if live(vu, UNITS):
                        wait(act, v_ready, vu + 1)
                        if v == LAG:
                            wait(act, o_ready, (s - 1) * SLOTS)
                        act.copy(V[0:KW, vpar, vv // 2, 512 * (vv % 2):512 * (vv % 2 + 1)],
                                 VT_ps[0:KW, :]).then_inc(v_evac, 1)
                    if v == 7 and live(f, STEPS):
                        gelus(f, par, [2])
                    if live(a, UNITS):
                        wait(act, sub_done, a + 1)
                        act.activation(E[:, v % 4, :, :], E[:, v % 4, :, :], ACT.Exp).then_inc(exp_done, 1)
                    a2 = a - 2
                    if live(a2, UNITS):
                        wait(act, pt_ready, a2 + 1)
                        wait(act, o_ready, a2 - 1)
                        act.copy(PT[:, (v - 2) % 2, :, :], PT_ps[0:KW, :].rearrange("p (m q) -> p m q", m=QB))\
                           .then_inc(pt_evac, 1)
                    a3 = a - 3
                    if live(a3, UNITS):
                        wait(act, o_ready, a3 + 1)
                        act.copy(OT[:, 1 - par if v >= 3 else par, (v - 3) % SLOTS, :], O_ps[:, 0:N])\
                           .then_inc(o_evac, 1)
                    if live(vu, UNITS):
                        half, tile, kind = vv // 4, (vv // 2) % 2, vv % 2
                        wait(act, tr_ready, vu + 1)
                        if v == LAG:
                            wait(act, s_ready, (s - 1) * SLOTS)
                        if kind == 0:
                            for h in range(2):
                                act.copy(QT[64 * h:64 * h + 64, vpar, 4 * half:4 * half + 4, 2 * tile:2 * tile + 2, h, :],
                                         VT_ps[64 * h:64 * h + 64, :].rearrange("p (i m q) -> p i m q", i=4, m=2))\
                                   .then_inc(tr_evac, 1)
                        else:
                            act.copy(KT[:, vpar, 4 * half:4 * half + 4, PAD + P * tile:PAD + P * (tile + 1)],
                                     VT_ps[:, :].rearrange("p (i q) -> p i q", i=4)).then_inc(tr_evac, 2)
                    if v == 4 and live(f, STEPS):
                        wait(act, mid_done, f + 1)
                        act.copy(xs[0:64, :], xm[0:64, par, :]).then_inc(xs_done, 1)
                        act.copy(xs[64:P, 1:N], xm[64:P, par, 0:N - 1]).then_inc(xs_done, 1)
                    if v == 5 and live(f, STEPS):
                        wait(act, cent_done, f + 1)
                        act.activation(xq[:, :], xc[:, :], ACT.Square).then_inc(xq_done, 1)
                    if v == 5 and live(s + 1, STEPS):
                        wait(act, qk_ready, s * SLOTS)
                        wait(act, v_ready, s * SLOTS)
                        stage(s + 1, 1 - par)

            def gelus(f, par, chunks):
                for r_ in chunks:
                    w = FCH[r_][1]
                    wait(act, ff_ready, f * FF_USES + K_W1 + r_ + 1)
                    act.activation(gel[0:w, r_, :], F_ps[(par + K_W1 + r_) % 2][0:w, N:2 * N], ACT.Gelu,
                                   bias=prm[0:w, R_B1G + r_:R_B1G + r_ + 1]).then_inc(gel_done, 1)

            all_steps(act, step)
            for c in range(4):
                act.wait_ge(ff_final, STEPS - 6 + 2 * c if c < 3 else STEPS)
                act.activation(xT[:, 2 * c:2 * c + 2, :], xT[:, 2 * c:2 * c + 2, :], ACT.Silu).then_inc(g_done, 1)

        @block.vector
        def _(dve):
            dve.memset(eps[:, :], 1e-5).then_inc(set_dve, 1)
            dve.memset(mean_w[:, :], 1.0 / D).then_inc(set_dve, 1)
            dve.wait_ge(in_cst, 16)
            dve.tensor_copy(ident_bf[:, :], ident).then_inc(set_dve, 1)
            dve.tensor_copy(mask_bf[:, :], cst[:, C_MASK:C_MASK + QB * KW]).then_inc(set_dve, 1)
            dve.wait_ge(in_x, 16)
            for t in range(TILES):
                dve.bn_stats(stats[:, t, :], x_tok[:, t, :]).then_inc(st_done, 1)
            for t in range(TILES):
                dve.wait_ge(st_done, t + 1)
                dve.bn_aggr(mv[:, t, :], stats[:, t, :]).then_inc(mv_done, 1)
            dve.wait_ge(sd_done, 1)
            dve.reciprocal(rst[:, :], rst[:, :]).then_inc(sd_done, 1)
            dve.wait_ge(sd_done, 2)
            dve.wait_ge(mv_done, TILES)
            for t in range(TILES):
                dve.tensor_scalar(x_tok[:, t, :], x_tok[:, t, :], mv[:, t, 0:1], rst[:, t:t + 1],
                                  ALU.subtract, ALU.mult).then_inc(ln_done, 1)
            for c in range(4):
                dve.wait_ge(rec_act, 4 + c + 1)
                dve.tensor_tensor(G[:, 512 * c:512 * (c + 1)], U[:, 512 * c:512 * (c + 1)],
                                  G[:, 512 * c:512 * (c + 1)], ALU.mult).then_inc(u_done, 1)
            for c in range(4):
                dve.wait_ge(uB_ready, c + 1)
                dve.wait_ge(u_done, 4)
                dve.tensor_copy(U[:, 512 * c:512 * (c + 1)], banks[c][:, :]).then_inc(Z_done, 1)
            k, r = 1, 0
            while k < N:
                if 2 * k < N:
                    pass
                for c in range(4):
                    dve.wait_ge(scan_ready, 4 * r + c + 1)
                    dve.wait_ge(Z_done, 4 * r + c + 1)
                    zc = Z[:, 2 * c:2 * c + 2, k:N]
                    dve.tensor_tensor(zc, zc, banks[c][:, 0:2 * (N - k)].rearrange("p (b n) -> p b n", b=2),
                                      ALU.add).then_inc(Z_done, 1)
                if 2 * k < N:
                    dve.wait_ge(pow_ready, r + 1)
                    dve.tensor_copy(powA[:, (r + 1) % 2, :, :].rearrange("p a n -> p (a n)"),
                                    banks[4 + r % 2][:, 0:2 * P]).then_inc(pow_done, 1)
                k, r = 2 * k, r + 1
            yf = yT[:, :, :].rearrange("p b n -> p (b n)")
            for c in range(4):
                dve.wait_ge(scan_ready, 4 * r + c + 1)
                dve.tensor_scalar(yf[:, 512 * c:512 * (c + 1)], banks[4 + c][:, :], rb[:, 2:3], None,
                                  ALU.add).then_inc(yT_done, 1)
            dve.wait_ge(in_scl, 16)

            def step(s, par):
                if par == 0 and live(s, STEPS):
                    l = s // B
                    for kind in range(2):
                        for cs in range(2):
                            base = cst[:, C_TAB + (2 * kind + cs) * NT * DH:C_TAB + (2 * kind + cs + 1) * NT * DH]\
                                .rearrange("p (t d) -> p t d", t=NT)
                            scl = scales[:, 2 * kind + cs, bass.ds(l, 1), :] if not isinstance(s, int) else \
                                scales[:, 2 * kind + cs, l:l + 1, :]
                            dve.tensor_tensor(table[:, kind, cs, :, :], base, scl.to_broadcast([P, NT, DH]),
                                              ALU.mult).then_inc(tab_done, 1)
                for v in range(SLOTS):
                    g = s * SLOTS + v
                    a = g - SLOTS
                    f = s - 2
                    if live(a - 1, UNITS):
                        wait(dve, exp_done, a)
                        dve.tensor_reduce(sm[:, (v - 1) % 4, :], E[:, (v - 1) % 4, :, :], AX_X, ALU.add)\
                           .then_inc(sum_done, 1)
                        wait(dve, sum_done, a)
                        wait(dve, p_norm, a - 4)
                        dve.reciprocal(rs[:, (v - 1) % 4, :], sm[:, (v - 1) % 4, :]).then_inc(rs_done, 1)
                    if v == 7 and live(f, STEPS):
                        hidden(f, par, [0, 1])
                    if v == 4 and live(f, STEPS):
                        b = f % B
                        xb = xT[:, b, :] if isinstance(f, int) else \
                            xT[:, bass.ds(b, 1), :].rearrange("p o n -> p (o n)")
                        wait(dve, ff_ready, f * FF_USES + K_WO + 1)
                        dve.tensor_tensor(xm[:, par, :], F_ps[(par + K_WO) % 2][:, 0:N], xb, ALU.add)\
                           .then_inc(mid_done, 1)
                    if v == 5 and live(f, STEPS):
                        wait(dve, ff_ready, f * FF_USES + K_MEAN + 1)
                        wait(dve, xs_done, 2 * (f + 1))
                        dve.tensor_tensor(xc[:, :], xs[:, :], F_ps[(par + K_MEAN) % 2][:, 0:N], ALU.subtract)\
                           .then_inc(cent_done, 1)
                    if live(g, UNITS):
                        half, tile, kind = v // 4, (v // 2) % 2, v % 2
                        if v == 0 and par == 0:
                            wait(dve, tab_done, 4 * (s // 2 + 1))
                        q8 = QK_ps[:, :].rearrange("p (h c d) -> p h c d", h=8, c=2)
                        tab = table[:, kind, :, tile, :].rearrange("p a (c d) -> p a c d", c=2)
                        wait(dve, sq_done, g + 1)
                        wait(dve, tr_ready, g - 3)
                        dve.tensor_tensor(t1[:, v % 4, :].rearrange("p (h d) -> p h d", h=8),
                                          QK_ps[:, :].rearrange("p (h d) -> p h d", h=8),
                                          table[:, kind, 0, tile, :].unsqueeze(1).to_broadcast([P, 8, DH]),
                                          ALU.mult).then_inc(t12_done, 1)
                        wait(dve, add_done, g - 1)
                        dve.tensor_tensor(t2[:, v % 2, :].rearrange("p (h c d) -> p h c d", h=8, c=2),
                                          q8[:, :, ::-1, :],
                                          tab[:, 1].unsqueeze(1).to_broadcast([P, 8, 2, DH // 2]),
                                          ALU.mult).then_inc(t12_done, 1)
                    if live(a, UNITS):
                        wait(dve, s_ready, a + 1)
                        Sv = S_ps[v % 2][:, 0:QB * KW].rearrange("p (m k) -> p m k", m=QB)
                        dve.tensor_reduce(mx[:, v % 2, :], Sv, AX_X, ALU.max).then_inc(max_done, 1)
                        wait(dve, max_done, a + 1)
                        wait(dve, pt_ready, a - 3)
                        dve.tensor_tensor(E[:, v % 4, :, :], Sv, mx[:, v % 2, :].unsqueeze(2).to_broadcast([P, QB, KW]),
                                          ALU.subtract).then_inc(sub_done, 1)
                    if live(g, UNITS):
                        wait(dve, sq_done, g + 1)
                        dve.tensor_reduce(ss[:, (v // 2) % 2, 8 * (v % 2):8 * (v % 2) + 8],
                                          sq[:, v % 2, :].rearrange("p (h d) -> p h d", h=8), AX_X, ALU.add)\
                           .then_inc(ss_done, 1)
                    if v % 2 == 1 and live(g, UNITS):
                        pair, i = s * 4 + v // 2, (v // 2) % 2
                        wait(dve, ss_done, g + 1)
                        wait(dve, nw_seq, (pair - 1) * NW_OPS)
                        dve.tensor_scalar(hss[:, i, :], ss[:, i, :], 1e-24, 0.5, ALU.max, ALU.mult)\
                           .then_inc(seed_done, 1)
                        wait(dve, seed_done, 2 * pair + 1)
                        wait(dve, qk_norm, g - 3)
                        dve.tensor_scalar(rn[:, i, :].bitcast(I32), hss[:, i, :].bitcast(I32), -0.5, RSQRT_SEED,
                                          ALU.mult, ALU.add).then_inc(seed_done, 1)
                    if v == 6 and live(f, STEPS):
                        wait(dve, std_done, f + 1)
                        dve.reciprocal(rstd[:, :], std[:, :]).then_inc(rstd_done, 1)
                        wait(dve, rstd_done, f + 1)
                        dve.tensor_tensor(xr[:, :], xc[:, :], rstd[:, :], ALU.mult).then_inc(xr_done, 1)
                        if par == 0:
                            wait(dve, in_ffn, (f // B + 1) * 48)
                        wait(dve, xr_done, f + 1)
                        dve.tensor_scalar(xn[:, :], xr[:, :], prm[:, R_G:R_G + 1], prm[:, R_B:R_B + 1],
                                          ALU.mult, ALU.add).then_inc(xn_done, 1)
                    if v == 7 and live(f, STEPS):
                        hidden(f, par, [2])
                    if v == 2 and live(s - 3, STEPS):
                        finish(s - 3, 1 - par)

            def hidden(f, par, chunks):
                for r_ in chunks:
                    w = FCH[r_][1]
                    wait(dve, gel_done, f * NCH + r_ + 1)
                    dve.scalar_tensor_tensor(out=hid[0:w, r_, :], in0=F_ps[(par + K_W1 + r_) % 2][0:w, 0:N],
                                             scalar=prm[0:w, R_B1A + r_:R_B1A + r_ + 1], in1=gel[0:w, r_, :],
                                             op0=ALU.add, op1=ALU.mult).then_inc(hid_done, 1)

            def finish(f, par):
                b = f % B
                xb = xT[:, b, :] if isinstance(f, int) else xT[:, bass.ds(b, 1), :].rearrange("p o n -> p (o n)")
                wait(dve, ff_ready, (f + 1) * FF_USES)
                wait(dve, mid_done, f + 1)
                dve.scalar_tensor_tensor(out=xb, in0=F_ps[(par + K_W2) % 2][:, 0:N], scalar=prm[:, R_B2:R_B2 + 1],
                                         in1=xm[:, par, :], op0=ALU.add, op1=ALU.add).then_inc(ff_final, 1)

            all_steps(dve, step)
            finish(STEPS - 1, (STEPS - 1) % 2)
            for c in range(4):
                dve.wait_ge(g_done, c + 1)
                yc = yT[:, 2 * c:2 * c + 2, :]
                dve.tensor_tensor(yc, yc, xT[:, 2 * c:2 * c + 2, :], ALU.mult).then_inc(prod_done, 1)
            dve.wait_ge(in_x2, 16)
            for c in range(4):
                dve.wait_ge(oT_ready, c + 1)
                dve.tensor_tensor(o_tok[:, 4 * c:4 * c + 4, :], banks[c][:, :].rearrange("p (t d) -> p t d", t=4),
                                  x_tok[:, 4 * c:4 * c + 4, :], ALU.add).then_inc(o_done, 1)

        @block.gpsimd
        def _(pool):
            pool.memset(QT[:, :, :, :, :, :].rearrange("p a b c d e -> p (a b c d e)"), 0.0).then_inc(set_pool, 1)
            pool.memset(KT[:, :, :, 0:PAD], 0.0).then_inc(set_pool, 1)
            pool.memset(xw[:, :, 0:PAD + 1], 0.0).then_inc(set_pool, 1)
            pool.memset(hid[:, NCH - 1, :], 0.0).then_inc(set_pool, 1)
            pool.memset(xs[:, 0:1], 0.0).then_inc(set_pool, 1)
            pool.memset(c15[:, :], 1.5).then_inc(set_pool, 1)
            pool.wait_ge(set_pool, 6)

            def step(s, par):
                for v in range(SLOTS):
                    g = s * SLOTS + v
                    a = g - SLOTS
                    if live(a - 1, UNITS):
                        wait(pool, rs_done, a)
                        pool.tensor_tensor(E[:, (v - 1) % 4, :, :], E[:, (v - 1) % 4, :, :],
                                           rs[:, (v - 1) % 4, :].unsqueeze(2).to_broadcast([P, QB, KW]),
                                           ALU.mult).then_inc(p_norm, 1)
                    if live(g, UNITS):
                        wait(pool, t12_done, 2 * (g + 1))
                        pool.tensor_tensor(t1[:, v % 4, :], t1[:, v % 4, :], t2[:, v % 2, :], ALU.add)\
                            .then_inc(add_done, 1)
                    if v % 2 == 1 and live(g, UNITS):
                        pair = s * 4 + v // 2
                        i = (v // 2) % 2
                        seq = pair * NW_OPS
                        wait(pool, seed_done, 2 * (pair + 1))
                        for n in range(NEWTON):
                            wait(pool, nw_seq, seq + 4 * n + 0)
                            pool.tensor_tensor(nwt[:, :], rn[:, i, :], rn[:, i, :], ALU.mult).then_inc(nw_seq, 1)
                            wait(pool, nw_seq, seq + 4 * n + 1)
                            pool.tensor_tensor(nwt[:, :], nwt[:, :], hss[:, i, :], ALU.mult).then_inc(nw_seq, 1)
                            wait(pool, nw_seq, seq + 4 * n + 2)
                            pool.tensor_tensor(nwt[:, :], c15[:, :], nwt[:, :], ALU.subtract).then_inc(nw_seq, 1)
                            wait(pool, nw_seq, seq + 4 * n + 3)
                            pool.tensor_tensor(rn[:, i, :], rn[:, i, :], nwt[:, :], ALU.mult).then_inc(nw_seq, 1)
                        wait(pool, nw_seq, seq + NW_OPS)
                        wait(pool, add_done, g + 1)
                        for e in range(2):
                            w = t1[:, (v - 1 + e) % 4, :].rearrange("p (h d) -> p h d", h=8)
                            pool.tensor_tensor(w, w, rn[:, i, 8 * e:8 * e + 8].unsqueeze(2).to_broadcast([P, 8, DH]),
                                               ALU.mult).then_inc(qk_norm, 1)

            all_steps(pool, step)


def shape_constants():
    c = np.zeros((P, C_ALL), np.float32)
    c[:, C_ID:C_ID + P] = np.eye(P, dtype=np.float32)
    q = np.arange(P)[:, None] % 64
    k = np.arange(KW)[None, :]
    allowed = (k >= q) & (k <= q + WINDOW)
    for m in range(QB):
        ok = allowed & (k >= WINDOW) if m == 0 else allowed
        c[:, C_MASK + KW * m:C_MASK + KW * (m + 1)] = np.where(ok, 0.0, -1e30)
    half = np.arange(0, DH, 2, dtype=np.float32)
    inv_freq = (1.0 / np.float32(10000.0) ** (half / DH)).astype(np.float32)
    t = np.arange(N, dtype=np.float32)
    freqs = t[:, None] * inv_freq[None, :]
    freqs = np.concatenate([freqs, freqs], -1)
    base = (half + np.float32(0.4 * DH)) / np.float32(1.4 * DH)
    power = (t - N // 2) / (WINDOW // 2)
    scale = (base[None, :] ** power[:, None]).astype(np.float32)
    scale = np.concatenate([scale, scale], -1)
    sign = np.where(np.arange(DH) < DH // 2, -1.0, 1.0).astype(np.float32)
    cos, sin = np.cos(freqs), np.sin(freqs) * sign
    for i, tab in enumerate((QK_SCALE * cos * scale, QK_SCALE * sin * scale, cos / scale, sin / scale)):
        c[:, C_TAB + i * NT * DH:C_TAB + (i + 1) * NT * DH] = \
            tab.reshape(NT, P, DH).transpose(1, 0, 2).reshape(P, NT * DH).astype(np.float32)
    return c


def kernel(**inputs):
    import concourse.bacc as bacc
    from concourse.bass_utils import run_bass_kernel_spmd

    i = {k: np.asarray(v) for k, v in inputs.items()}

    def cols(a, n):
        a = np.concatenate([a, np.zeros((DEPTH, n * P - a.shape[1]), a.dtype)], 1)
        return a.reshape(DEPTH, n, P).transpose(0, 2, 1)

    qs, ks = i["L0_ffn_q_scale"], i["L0_ffn_k_scale"]
    swap = np.concatenate([np.arange(DH // 2, DH), np.arange(DH // 2)])
    w2 = i["L0_ffn_W2"]
    w2 = np.concatenate([w2, np.zeros((DEPTH, NCH * P - FF, D), w2.dtype)], 1)
    b1 = i["L0_ffn_b1"]
    arrays = {
        "x": i["L0_attn_x"],
        "rec_w": np.stack([i["L0_attn_W_u"].T, i["L0_attn_W_g"].T, i["L0_attn_A"], i["L0_attn_A"].T,
                           i["L0_attn_Bm"].T, i["L0_attn_Cm"].T], 1),
        "rec_b": np.stack([i["L0_attn_b_u"], i["L0_attn_b_g"], i["L0_attn_D"]], 1),
        "wqkv": i["L0_ffn_Wqkv"],
        "wo": i["L0_ffn_Wo"].reshape(DEPTH, HP, P, D).transpose(0, 2, 1, 3),
        "w1": i["L0_ffn_W1"],
        "w2": w2.reshape(DEPTH, NCH, P, D).transpose(0, 2, 1, 3),
        "params": np.concatenate([cols(i["L0_ffn_ln_g"], 1), cols(i["L0_ffn_ln_b"], 1), cols(b1[:, :FF], NCH),
                                  cols(b1[:, FF:], NCH), cols(i["L0_ffn_b2"], 1)], 2),
        "qk_scales": np.broadcast_to(np.stack([qs, qs[:, swap], ks, ks[:, swap]])[None], (P, 4, DEPTH, DH)),
        "consts": shape_constants(),
    }
    arrays = {k: np.ascontiguousarray(v) for k, v in arrays.items()}
    nc = bacc.Bacc("TRN2", target_bir_lowering=False, num_devices=1)
    aps = {k: nc.dram_tensor(f"in_{k}", v.shape, mybir.dt.from_np(v.dtype), kind="ExternalInput").ap()
           for k, v in arrays.items()}
    out = nc.dram_tensor("out", i["L0_attn_x"].shape, F32, kind="ExternalOutput").ap()
    gated_mix_kernel(nc, aps["x"], aps["rec_w"], aps["rec_b"], aps["wqkv"], aps["wo"], aps["w1"], aps["w2"],
                     aps["params"], aps["qk_scales"], aps["consts"], out)
    r = run_bass_kernel_spmd(nc, [{f"in_{k}": v for k, v in arrays.items()}], core_ids=[0])
    return r.results[0]["out"]
```

```python
from contextlib import ExitStack

import numpy as np

import concourse.bass as bass
from concourse import mybir

F32 = mybir.dt.float32
BF16 = mybir.dt.bfloat16
I32 = mybir.dt.int32
ALU = mybir.AluOpType
ACT = mybir.ActivationFunctionType
AX_X = mybir.AxisListType.X

P = 128
B, N, D = 8, 256, 128
DEPTH, HEADS, DH, WINDOW = 6, 16, 64, 32
INNER = HEADS * DH
FF = int(D * 4 * 2 / 3)
FCH = [(c * P, min(P, FF - c * P)) for c in range(-(-FF // P))]
NCH = len(FCH)
QK_SCALE = 8.0
STEPS = DEPTH * B
NORMS = 4 * 8
SLOTS = 8
UNITS = STEPS * SLOTS
HP = HEADS // 2
QB = N // 64
KW = 96
PAD = WINDOW
NT = N // P
T = B * N
TILES = T // P
L_SCALE, L_TR = 4, 5
L_S = L_TR + 4
L_EXP, L_RS, L_NORM, L_PT, L_PV = L_S + 1, L_S + 2, L_S + 2, L_S + 3, L_S + 4
L_V = L_PV - SLOTS
F_WO = L_PV + SLOTS + 1
F_MID, F_MEAN, F_CENT, F_VAR = (F_WO + i for i in (1, 2, 2, 3))
F_VCOPY = F_VAR + 1 + (SLOTS // 2 - 1 - (F_VAR + 1) % (SLOTS // 2))
F_BC, F_XN, F_W1, F_GEL, F_W2, F_END = (F_VCOPY + i for i in (1, 1, 2, 3, 4, 5))
RSQRT_SEED = float(0x5F1FFFF9)
LEAD = 4
NEWTON = ((0.703952253, 0.703952253 * 2.38924456), (0.5, 1.5))
C_ID, C_MASK, C_TAB = 0, P, P + QB * KW
C_ALL = C_TAB + 4 * NT * DH
R_G, R_B, R_B1A, R_B1G, R_B2 = 0, 1, 2, 2 + NCH, 2 + 2 * NCH
R_ALL = 3 + 2 * NCH


def live(unit, count):
    return 0 <= unit < count if isinstance(unit, int) else True


def unit(s, par, v, lag):
    back = (v - lag) // SLOTS
    return s * SLOTS + v - lag, (v - lag) % SLOTS, s + back, (par + back) % 2


def batch(s, par, v, lag):
    back = (v - lag) // SLOTS
    here = (v - lag) % SLOTS == 0 and live(s + back, STEPS)
    return (s + back if here else None), (par + back) % 2


def upto(count, most):
    return min(count, most) if isinstance(count, int) else count


def wait(eng, sem, count):
    if not isinstance(count, int) or count > 0:
        eng.wait_ge(sem, count)


def all_steps(eng, step):
    for s in range(LEAD):
        step(s, s % 2)
    with eng.Fori(LEAD // 2, STEPS // 2) as j:
        step(2 * j, 0)
        step(2 * j + 1, 1)
    for s in range(STEPS, STEPS + LEAD):
        step(s, s % 2)


def gated_mix_kernel(nc, x, rec_w, rec_b, wqkv, wo, w1, w2, params, qk_scales, consts, out):
    with ExitStack() as ctx:
        def sb(name, shape, dt=F32):
            return ctx.enter_context(nc.sbuf_tensor(name, shape, dt))

        def sem(name):
            return ctx.enter_context(nc.semaphore(name))

        cst = sb("cst", [P, C_ALL])
        ident = cst[:, C_ID:C_ID + P]
        ident_bf = sb("ident_bf", [P, P], BF16)
        mask_bf = sb("mask_bf", [P, QB * KW], BF16)
        mean_w = sb("mean_w", [P, P])
        ones = sb("ones", [P, P])
        scales = sb("scales", [P, 4, DEPTH, DH])
        wqkv_sb = sb("wqkv_sb", [P, 3 * INNER])
        wo_sb = sb("wo_sb", [P, HP, D])
        w1_sb = sb("w1_sb", [P, 2 * FF])
        w2_sb = sb("w2_sb", [P, NCH, D])
        prm = sb("prm", [P, R_ALL])
        xT = sb("xT", [P, B, N])
        yT = sb("yT", [P, B, N])
        xw = sb("xw", [P, 2, PAD + N])
        table = sb("table", [P, 2, 2, NT, DH])
        sq = sb("sq", [P, 2, 512])
        t1 = sb("t1", [P, 8, 512])
        t2 = sb("t2", [P, 2, 512])
        ss = sb("ss", [P, 2, NORMS + NT])
        rn = sb("rn", [P, 2, NORMS + NT])
        nwt = sb("nwt", [P, NORMS + NT])
        QT = sb("QT", [P, 2, HP, QB, 2, 64])
        KT = sb("KT", [P, 2, HP, PAD + N])
        V = sb("V", [P, 2, QB, INNER])
        nmx = sb("nmx", [P, 2, QB])
        sm = sb("sm", [P, 4, QB])
        rs = sb("rs", [P, 4, QB])
        E = sb("E", [P, 4, QB, KW])
        PT = sb("PT", [KW, 2, QB, P])
        OT = sb("OT", [P, 2, HP, N])
        xm = sb("xm", [P, 2, N])
        xs = sb("xs", [P, N])
        xc = sb("xc", [P, N])
        xq = sb("xq", [P, N])
        diag = sb("diag", [P, NT, P])
        xr = sb("xr", [P, N])
        xn = sb("xn", [P, N])
        gel = sb("gel", [P, NCH, N])
        hid = sb("hid", [P, NCH, N])
        x_tok = V[:, 0, 0:2, :].rearrange("p a b -> p (a b)").rearrange("p (t d) -> p t d", d=D)
        o_tok = V[:, 0, 2:4, :].rearrange("p a b -> p (a b)").rearrange("p (t d) -> p t d", d=D)
        U = V[:, 1, 0:2, :].rearrange("p a b -> p (a b)")
        G = V[:, 1, 2:4, :].rearrange("p a b -> p (a b)")
        Z = U.rearrange("p (b n) -> p b n", b=B)
        rw = sb("rw", [P, 6, P])
        rb = sb("rb", [P, 3])
        powA = sb("powA", [P, 2, 2, P])
        stats = sb("stats", [P, TILES, 6])
        mv = sb("mv", [P, TILES, 2])
        rst = sb("rst", [P, TILES])
        eps = sb("eps", [P, 1])

        def bank(name):
            return ctx.enter_context(nc.psum_tensor(name, [P, 512], F32))

        S_ps = [bank("S0"), bank("S1")]
        PT_ps = bank("PTb")
        O_ps = bank("Ob")
        F_ps = [bank("F0"), bank("F1")]
        QK_ps = bank("QKb")
        VT_ps = bank("VTb")
        banks = [S_ps[0], S_ps[1], PT_ps, O_ps, F_ps[0], F_ps[1], QK_ps, VT_ps]

        in_x, in_rec, in_cst, in_scl = sem("in_x"), sem("in_rec"), sem("in_cst"), sem("in_scl")
        in_wqk, in_wv, in_wo, in_ffn = sem("in_wqk"), sem("in_wv"), sem("in_wo"), sem("in_ffn")
        set_pool, set_dve = sem("set_pool"), sem("set_dve")
        st_done, mv_done, sd_done, ln_done, lnT_ready, xT_done = (
            sem("st_done"), sem("mv_done"), sem("sd_done"), sem("ln_done"), sem("lnT_ready"), sem("xT_done"))
        rec_mm, rec_act, u_done, uB_ready, Z_done, pow_ready, pow_done, yT_done = (
            sem("rec_mm"), sem("rec_act"), sem("u_done"), sem("uB_ready"), sem("Z_done"), sem("pow_ready"),
            sem("pow_done"), sem("yT_done"))
        scan_ready = sem("scan_ready")
        x_staged, tab_done = sem("x_staged"), sem("tab_done")
        qk_ready, sq_done, t12_done, ss_done = sem("qk_ready"), sem("sq_done"), sem("t12_done"), sem("ss_done")
        add_done, nw_seq, qk_norm = sem("add_done"), sem("nw_seq"), sem("qk_norm")
        tr_ready, tr_evac, v_ready, v_evac = sem("tr_ready"), sem("tr_evac"), sem("v_ready"), sem("v_evac")
        s_ready, max_done, exp_done = sem("s_ready"), sem("max_done"), sem("exp_done")
        rs_done, p_norm = sem("rs_done"), sem("p_norm")
        pt_ready, pt_evac, o_ready, o_evac = sem("pt_ready"), sem("pt_evac"), sem("o_ready"), sem("o_evac")
        wo_ready, mean_ready, var_ready, bc_ready, w1_ready, w2_ready = (
            sem("wo_ready"), sem("mean_ready"), sem("var_ready"), sem("bc_ready"), sem("w1_ready"), sem("w2_ready"))
        mid_done, xs_done, cent_done, xq_done = (
            sem("mid_done"), sem("xs_done"), sem("cent_done"), sem("xq_done"))
        var_copied, diag_done, xr_done, xn_done, gel_done, hid_done, ff_final = (
            sem("var_copied"), sem("diag_done"), sem("xr_done"), sem("xn_done"), sem("gel_done"), sem("hid_done"),
            sem("ff_final"))
        g_done, prod_done, oT_ready, o_done, stored = (
            sem("g_done"), sem("prod_done"), sem("oT_ready"), sem("o_done"), sem("stored"))
        in_x2 = sem("in_x2")

        BANK_WO, BANK_W2, BANK_MEAN, BANK_VAR, BANK_BC = (F_ps[i] for i in (0, 1, 0, 1, 0))
        BANK_W1 = [F_ps[1], F_ps[0], F_ps[1]]
        NW_OPS = 2 + 3 * len(NEWTON)

        LN_HALF = (F_VCOPY % SLOTS) // 4

        def newton_count(s, half):
            if isinstance(s, int) and s >= STEPS:
                return (2 * STEPS + s - STEPS + 1) * NW_OPS
            return (2 * s + half + 1) * NW_OPS

        def ln_newton(s, v):
            return s + (v - 1) // SLOTS, LN_HALF

        block = ctx.enter_context(nc.Block())

        @block.sync
        def _(sp):
            sp.dma_start(x_tok, x.rearrange("b (t p) d -> p (b t) d", p=P)).then_inc(in_x, 16)
            sp.dma_start(cst[:, :], consts).then_inc(in_cst, 16)
            sp.dma_start(rw[:, :, :], rec_w).then_inc(in_rec, 16)
            sp.dma_start(rb[:, :], rec_b).then_inc(in_rec, 16)
            sp.dma_start(wqkv_sb[:, 0:2 * INNER], wqkv[0, :, 0:2 * INNER]).then_inc(in_wqk, 16)
            sp.dma_start(wqkv_sb[:, 2 * INNER:], wqkv[0, :, 2 * INNER:]).then_inc(in_wv, 16)
            sp.dma_start(scales[:, :, :, :], qk_scales).then_inc(in_scl, 16)
            sp.dma_start(wo_sb[:, :, :], wo[0]).then_inc(in_wo, 16)
            sp.dma_start(w1_sb[:, :], w1[0]).then_inc(in_ffn, 16)
            sp.dma_start(w2_sb[:, :, :], w2[0]).then_inc(in_ffn, 16)
            sp.dma_start(prm[:, :], params[0]).then_inc(in_ffn, 16)
            with sp.Fori(1, DEPTH) as l:
                w_l = wqkv[bass.ds(l, 1)].rearrange("o p n -> (o p) n")
                sp.wait_ge(qk_ready, l * (B * SLOTS))
                sp.dma_start(wqkv_sb[:, 0:2 * INNER], w_l[:, 0:2 * INNER]).then_inc(in_wqk, 16)
                sp.wait_ge(v_ready, l * (B * SLOTS))
                sp.dma_start(wqkv_sb[:, 2 * INNER:], w_l[:, 2 * INNER:]).then_inc(in_wv, 16)
                sp.wait_ge(wo_ready, l * B)
                sp.dma_start(wo_sb[:, :, :], wo[bass.ds(l, 1)].rearrange("o p h n -> (o p) h n")).then_inc(in_wo, 16)
                sp.wait_ge(ff_final, l * B)
                sp.dma_start(w1_sb[:, :], w1[bass.ds(l, 1)].rearrange("o p n -> (o p) n")).then_inc(in_ffn, 16)
                sp.dma_start(w2_sb[:, :, :], w2[bass.ds(l, 1)].rearrange("o p c n -> (o p) c n")).then_inc(in_ffn, 16)
                sp.dma_start(prm[:, :], params[bass.ds(l, 1)].rearrange("o p n -> (o p) n")).then_inc(in_ffn, 16)
            sp.wait_ge(o_ready, UNITS)
            sp.dma_start(x_tok, x.rearrange("b (t p) d -> p (b t) d", p=P)).then_inc(in_x2, 16)
            for c in range(4):
                sp.wait_ge(o_done, c + 1)
                sp.dma_start(out[2 * c:2 * c + 2].rearrange("b (t p) d -> p (b t) d", p=P),
                             o_tok[:, 4 * c:4 * c + 4, :]).then_inc(stored, 16)
            sp.wait_ge(stored, 64)

        @block.tensor
        def _(pe):
            pe.wait_ge(in_cst, 16)
            pe.wait_ge(in_rec, 32)
            for t in range(TILES):
                pe.wait_ge(ln_done, t + 1)
                mm = pe.transpose(banks[t // 4][:, (t % 4) * P:(t % 4 + 1) * P], x_tok[:, t, :], ident)
                if t % 4 == 3:
                    mm.then_inc(lnT_ready, 1)
            xf = xT[:, :, :].rearrange("p b n -> p (b n)")
            Zf = U
            for c in range(4):
                pe.wait_ge(xT_done, c + 1)
                for k in range(2):
                    pe.matmul(banks[4 * k + c][:, :], rw[:, k, :], xf[:, 512 * c:512 * (c + 1)],
                              start=True, stop=True).then_inc(rec_mm, 1)
            for c in range(4):
                pe.wait_ge(u_done, c + 1)
                pe.matmul(banks[c][:, :], rw[:, 4, :], G[:, 512 * c:512 * (c + 1)],
                          start=True, stop=True).then_inc(uB_ready, 1)
            k, r = 1, 0
            while k < N:
                at, a_ = (rw[:, 3, :], rw[:, 2, :]) if r == 0 else (powA[:, r % 2, 0, :], powA[:, r % 2, 1, :])
                if r:
                    pe.wait_ge(pow_done, r)
                for c in range(4):
                    pe.wait_ge(Z_done, 4 * r + c + 1)
                    pe.matmul(banks[c][:, 0:2 * (N - k)].rearrange("p (b n) -> p b n", b=2), at,
                              Z[:, 2 * c:2 * c + 2, 0:N - k], start=True, stop=True).then_inc(scan_ready, 1)
                if 2 * k < N:
                    pe.matmul(banks[4 + r % 2][:, 0:P], a_, at, start=True, stop=True)
                    pe.matmul(banks[4 + r % 2][:, P:2 * P], at, a_, start=True, stop=True).then_inc(pow_ready, 1)
                k, r = 2 * k, r + 1
            for c in range(4):
                pe.wait_ge(Z_done, 4 * r + c + 1)
                pe.matmul(banks[4 + c][:, :], rw[:, 5, :], Zf[:, 512 * c:512 * (c + 1)],
                          start=True, stop=True).then_inc(scan_ready, 1)
            pe.wait_ge(yT_done, 4)
            pe.wait_ge(set_pool, 5)
            pe.wait_ge(set_dve, 6)

            def step(s, par):
                for v in range(SLOTS):
                    g = s * SLOTS + v
                    if live(g, UNITS):
                        if v == 0:
                            if par == 0:
                                wait(pe, in_wqk, (s // B + 1) * 16)
                            wait(pe, x_staged, 2 * (s + 1))
                        wait(pe, t12_done, 2 * g)
                        half, tile, kind = v // 4, (v // 2) % 2, v % 2
                        pe.matmul(QK_ps[:, :], xw[:, par, PAD + P * tile:PAD + P * (tile + 1)],
                                  wqkv_sb[:, kind * INNER + 512 * half:kind * INNER + 512 * (half + 1)],
                                  start=True, stop=True).then_inc(qk_ready, 1)
                    u, vv, st, pr = unit(s, par, v, L_TR)
                    if live(u, UNITS):
                        wait(pe, qk_norm, u + 1)
                        wait(pe, v_evac, upto(g - L_V, UNITS))
                        wait(pe, tr_evac, 2 * u)
                        for i in range(4):
                            mm = pe.transpose(VT_ps[:, P * i:P * (i + 1)], t1[:, vv, P * i:P * (i + 1)], ident)
                        mm.then_inc(tr_ready, 1)
                    a, hp, st, pr = unit(s, par, v, L_S)
                    if live(a, UNITS):
                        if hp % 4 == 0:
                            wait(pe, tr_evac, 2 * (st * SLOTS + 4 * (hp // 4 + 1)))
                        wait(pe, exp_done, QB * (a - 1))
                        for m in range(QB):
                            pe.matmul(S_ps[hp % 2][:, KW * m:KW * (m + 1)],
                                      QT[:, pr, hp, m, :, :].rearrange("p h q -> p (h q)"),
                                      KT[:, pr, hp, 64 * m:64 * m + KW],
                                      start=(m == 0), stop=False, skip_group_check=True)
                        pe.matmul(S_ps[hp % 2][:, 0:QB * KW], ident_bf[:, :], mask_bf[:, :], start=False, stop=True,
                                  skip_group_check=True).then_inc(s_ready, 1)
                    f, pr = batch(s, par, v, F_MEAN)
                    if f is not None:
                        wait(pe, xs_done, 2 * (f + 1))
                        pe.matmul(BANK_MEAN[:, 0:N], mean_w[:, :], xs[:, :], start=True, stop=True)\
                          .then_inc(mean_ready, 1)
                    f, pr = batch(s, par, v, F_VAR)
                    if f is not None:
                        wait(pe, xq_done, f + 1)
                        wait(pe, ff_final, f)
                        for t in range(NT):
                            mm = pe.matmul(BANK_VAR[:, t:t + 1], xq[:, P * t:P * (t + 1)], mean_w[:, 0:1],
                                           start=True, stop=True)
                        mm.then_inc(var_ready, 1)
                    f, pr = batch(s, par, v, F_BC)
                    if f is not None:
                        wait(pe, diag_done, f + 1)
                        pe.matmul(BANK_BC[:, 0:N], ones[:, :], diag[:, :, :].rearrange("p t q -> p (t q)"),
                                  start=True, stop=True).then_inc(bc_ready, 1)
                    f, pr = batch(s, par, v, F_GEL)
                    if f is not None:
                        ff_w1(f, pr, [2])
                    a, hp, st, pr = unit(s, par, v, L_PT)
                    if live(a, UNITS):
                        wait(pe, p_norm, a + 1)
                        wait(pe, pt_evac, a)
                        for m in range(QB):
                            mm = pe.transpose(PT_ps[0:KW, P * m:P * (m + 1)], E[:, hp % 4, m, :], ident)
                        mm.then_inc(pt_ready, 1)
                    a, hp, st, pr = unit(s, par, v, L_PV)
                    if live(a, UNITS):
                        if hp == 0:
                            wait(pe, v_evac, (st + 1) * SLOTS)
                        wait(pe, pt_evac, a + 1)
                        wait(pe, o_evac, a)
                        for m in range(QB):
                            for h in range(2):
                                mm = pe.matmul(O_ps[64 * h:64 * h + 64, 64 * m:64 * m + 64],
                                               V[0:KW, pr, m, (2 * hp + h) * DH:(2 * hp + h + 1) * DH],
                                               PT[:, hp % 2, m, 64 * h:64 * h + 64], start=True, stop=True)
                        mm.then_inc(o_ready, 1)
                    u, vv, st, pr = unit(s, par, v, L_V)
                    if live(u, UNITS):
                        if vv == 0 and pr == 0:
                            wait(pe, in_wv, (st // B + 1) * 16)
                        if not live(g - L_TR, UNITS):
                            wait(pe, v_evac, u)
                        wait(pe, tr_evac, 2 * upto(g - L_TR + 1, UNITS))
                        m, half = vv // 2, vv % 2
                        pe.matmul(VT_ps[0:KW, :], xw[:, pr, 64 * m:64 * m + KW],
                                  wqkv_sb[:, 2 * INNER + 512 * half:2 * INNER + 512 * (half + 1)],
                                  start=True, stop=True).then_inc(v_ready, 1)
                    f, pr = batch(s, par, v, F_WO)
                    if f is not None:
                        if pr == 0:
                            wait(pe, in_wo, (f // B + 1) * 16)
                        wait(pe, hid_done, (f - 1) * NCH + 2)
                        wait(pe, o_evac, (f + 1) * SLOTS)
                        for h in range(HP):
                            mm = pe.matmul(BANK_WO[:, 0:N], wo_sb[:, h, :], OT[:, pr, h, :],
                                           start=(h == 0), stop=(h == HP - 1))
                        mm.then_inc(wo_ready, 1)
                    f, pr = batch(s, par, v, F_W1)
                    if f is not None:
                        if pr == 0:
                            wait(pe, in_ffn, (f // B + 1) * 48)
                        wait(pe, xn_done, f + 1)
                        ff_w1(f, pr, [0, 1])
                    f, pr = batch(s, par, v, F_W2)
                    if f is not None:
                        wait(pe, hid_done, (f + 1) * NCH)
                        for r_ in range(NCH):
                            mm = pe.matmul(BANK_W2[:, 0:N], w2_sb[:, r_, :], hid[:, r_, :],
                                           start=(r_ == 0), stop=(r_ == NCH - 1))
                        mm.then_inc(w2_ready, 1)

            def ff_w1(f, par, chunks):
                for r_ in chunks:
                    c0, w = FCH[r_]
                    fb = BANK_W1[r_]
                    if r_ == 2:
                        wait(pe, hid_done, f * NCH + 1)
                    pe.matmul(fb[0:w, 0:N], w1_sb[:, c0:c0 + w], xn[:, :], start=True, stop=True)
                    pe.matmul(fb[0:w, N:2 * N], w1_sb[:, FF + c0:FF + c0 + w], xn[:, :],
                              start=True, stop=True).then_inc(w1_ready, 1)

            all_steps(pe, step)
            for c in range(4):
                pe.wait_ge(prod_done, c + 1)
                for i in range(4):
                    mm = pe.transpose(banks[c][:, P * i:P * (i + 1)], yT[:, 2 * c + i // 2, (i % 2) * P:(i % 2 + 1) * P],
                                      ident)
                mm.then_inc(oT_ready, 1)

        @block.scalar
        def _(act):
            act.wait_ge(set_dve, 6)
            act.wait_ge(mv_done, TILES)
            act.activation(rst[:, :], mv[:, :, 1], ACT.Sqrt, bias=eps[:, 0:1]).then_inc(sd_done, 1)
            xf = xT[:, :, :].rearrange("p b n -> p (b n)")
            for c in range(4):
                act.wait_ge(lnT_ready, c + 1)
                act.copy(xf[:, 512 * c:512 * (c + 1)], banks[c][:, :]).then_inc(xT_done, 1)
            act.wait_ge(in_rec, 32)
            for c in range(4):
                act.wait_ge(rec_mm, 2 * c + 1)
                act.activation(U[:, 512 * c:512 * (c + 1)], banks[c][:, :], ACT.Gelu,
                               bias=rb[:, 0:1]).then_inc(rec_act, 1)
            for c in range(4):
                act.wait_ge(rec_mm, 2 * c + 2)
                act.activation(G[:, 512 * c:512 * (c + 1)], banks[4 + c][:, :], ACT.Sigmoid,
                               bias=rb[:, 1:2]).then_inc(rec_act, 1)

            def stage(s, par):
                b = s % B
                src = xT[:, b, :] if isinstance(s, int) else xT[:, bass.ds(b, 1), :].rearrange("p o n -> p (o n)")
                act.copy(xw[0:64, par, PAD:PAD + N], src[0:64, :]).then_inc(x_staged, 1)
                act.copy(xw[64:P, par, PAD + 1:PAD + N], src[64:P, 0:N - 1]).then_inc(x_staged, 1)

            act.wait_ge(xT_done, 4)
            act.wait_ge(yT_done, 4)
            act.wait_ge(set_pool, 5)
            stage(0, 0)

            def step(s, par):
                for v in range(SLOTS):
                    g = s * SLOTS + v
                    f, pr = batch(s, par, v, F_GEL)
                    if f is not None:
                        gelus(f, pr, [0, 1])
                    f, pr = batch(s, par, v, F_VAR)
                    if f is not None:
                        wait(act, cent_done, f + 1)
                        act.activation(xq[:, :], xc[:, :], ACT.Square).then_inc(xq_done, 1)
                    if live(g, UNITS):
                        wait(act, qk_ready, g + 1)
                        wait(act, ss_done, g - 1)
                        act.activation(sq[:, v % 2, :], QK_ps[:, :], ACT.Square).then_inc(sq_done, 1)
                    u, vv, st, pr = unit(s, par, v, L_TR)
                    if live(u, UNITS):
                        half, tile, kind = vv // 4, (vv // 2) % 2, vv % 2
                        wait(act, tr_ready, u + 1)
                        if vv % 4 == 0:
                            wait(act, s_ready, (st - 2) * SLOTS + 4 * (half + 1))
                        if kind == 0:
                            for h in range(2):
                                act.copy(QT[64 * h:64 * h + 64, pr, 4 * half:4 * half + 4, 2 * tile:2 * tile + 2, h, :],
                                         VT_ps[64 * h:64 * h + 64, :].rearrange("p (i m q) -> p i m q", i=4, m=2))\
                                   .then_inc(tr_evac, 1)
                        else:
                            act.copy(KT[:, pr, 4 * half:4 * half + 4, PAD + P * tile:PAD + P * (tile + 1)],
                                     VT_ps[:, :].rearrange("p (i q) -> p i q", i=4)).then_inc(tr_evac, 2)
                    f, pr = batch(s, par, v, F_GEL)
                    if f is not None:
                        gelus(f, pr, [2])
                    a, hp, st, pr = unit(s, par, v, L_EXP)
                    if live(a, UNITS):
                        wait(act, max_done, a + 1)
                        wait(act, pt_ready, a - 3)
                        for m in range(QB):
                            act.activation(E[:, hp % 4, m, :], S_ps[hp % 2][:, KW * m:KW * (m + 1)], ACT.Exp,
                                           bias=nmx[:, hp % 2, m:m + 1], accum_out=sm[:, hp % 4, m:m + 1])\
                               .then_inc(exp_done, 1)
                    a, hp, st, pr = unit(s, par, v, L_PT)
                    if live(a, UNITS):
                        wait(act, pt_ready, a + 1)
                        wait(act, o_ready, a - 1)
                        act.copy(PT[:, hp % 2, :, :], PT_ps[0:KW, :].rearrange("p (m q) -> p m q", m=QB))\
                           .then_inc(pt_evac, 1)
                    a, hp, st, pr = unit(s, par, v, L_PV)
                    if live(a, UNITS):
                        wait(act, o_ready, a + 1)
                        act.copy(OT[:, pr, hp, :], O_ps[:, 0:N]).then_inc(o_evac, 1)
                    f, pr = batch(s, par, v, F_MID)
                    if f is not None:
                        wait(act, mid_done, f + 1)
                        act.copy(xs[0:64, :], xm[0:64, pr, :]).then_inc(xs_done, 1)
                        act.copy(xs[64:P, 1:N], xm[64:P, pr, 0:N - 1]).then_inc(xs_done, 1)
                    if v == 6 and live(s + 1, STEPS):
                        wait(act, qk_ready, s * SLOTS)
                        wait(act, v_ready, s * SLOTS)
                        stage(s + 1, 1 - par)

            def gelus(f, par, chunks):
                for r_ in chunks:
                    w = FCH[r_][1]
                    wait(act, w1_ready, f * NCH + r_ + 1)
                    act.activation(gel[0:w, r_, :], BANK_W1[r_][0:w, N:2 * N], ACT.Gelu,
                                   bias=prm[0:w, R_B1G + r_:R_B1G + r_ + 1]).then_inc(gel_done, 1)

            all_steps(act, step)
            for c in range(4):
                act.wait_ge(ff_final, STEPS - 6 + 2 * c)
                act.activation(xT[:, 2 * c:2 * c + 2, :], xT[:, 2 * c:2 * c + 2, :], ACT.Silu).then_inc(g_done, 1)

        @block.vector
        def _(dve):
            dve.memset(eps[:, :], 1e-5).then_inc(set_dve, 1)
            dve.memset(mean_w[:, :], 1.0 / D).then_inc(set_dve, 1)
            dve.memset(ss[:, :, NORMS:], 1.0).then_inc(set_dve, 1)
            dve.memset(ones[:, :], 1.0).then_inc(set_dve, 1)
            dve.wait_ge(in_cst, 16)
            dve.tensor_copy(ident_bf[:, :], ident).then_inc(set_dve, 1)
            dve.tensor_copy(mask_bf[:, :], cst[:, C_MASK:C_MASK + QB * KW]).then_inc(set_dve, 1)
            dve.wait_ge(in_x, 16)
            for t in range(TILES):
                dve.bn_stats(stats[:, t, :], x_tok[:, t, :]).then_inc(st_done, 1)
            for t in range(TILES):
                dve.wait_ge(st_done, t + 1)
                dve.bn_aggr(mv[:, t, :], stats[:, t, :]).then_inc(mv_done, 1)
            dve.wait_ge(sd_done, 1)
            dve.reciprocal(rst[:, :], rst[:, :]).then_inc(sd_done, 1)
            dve.wait_ge(sd_done, 2)
            dve.wait_ge(mv_done, TILES)
            for t in range(TILES):
                dve.tensor_scalar(x_tok[:, t, :], x_tok[:, t, :], mv[:, t, 0:1], rst[:, t:t + 1],
                                  ALU.subtract, ALU.mult).then_inc(ln_done, 1)
            for c in range(4):
                dve.wait_ge(rec_act, 4 + c + 1)
                dve.tensor_tensor(G[:, 512 * c:512 * (c + 1)], U[:, 512 * c:512 * (c + 1)],
                                  G[:, 512 * c:512 * (c + 1)], ALU.mult).then_inc(u_done, 1)
            for c in range(4):
                dve.wait_ge(uB_ready, c + 1)
                dve.wait_ge(u_done, 4)
                dve.tensor_copy(U[:, 512 * c:512 * (c + 1)], banks[c][:, :]).then_inc(Z_done, 1)
            k, r = 1, 0
            while k < N:
                if 2 * k < N:
                    pass
                for c in range(4):
                    dve.wait_ge(scan_ready, 4 * r + c + 1)
                    dve.wait_ge(Z_done, 4 * r + c + 1)
                    zc = Z[:, 2 * c:2 * c + 2, k:N]
                    dve.tensor_tensor(zc, zc, banks[c][:, 0:2 * (N - k)].rearrange("p (b n) -> p b n", b=2),
                                      ALU.add).then_inc(Z_done, 1)
                if 2 * k < N:
                    dve.wait_ge(pow_ready, r + 1)
                    dve.tensor_copy(powA[:, (r + 1) % 2, :, :].rearrange("p a n -> p (a n)"),
                                    banks[4 + r % 2][:, 0:2 * P]).then_inc(pow_done, 1)
                k, r = 2 * k, r + 1
            yf = yT[:, :, :].rearrange("p b n -> p (b n)")
            for c in range(4):
                dve.wait_ge(scan_ready, 4 * r + c + 1)
                dve.tensor_scalar(yf[:, 512 * c:512 * (c + 1)], banks[4 + c][:, :], rb[:, 2:3], None,
                                  ALU.add).then_inc(yT_done, 1)
            dve.wait_ge(in_scl, 16)

            def step(s, par):
                if par == 0 and live(s, STEPS):
                    l = s // B
                    for kind in range(2):
                        for cs in range(2):
                            base = cst[:, C_TAB + (2 * kind + cs) * NT * DH:C_TAB + (2 * kind + cs + 1) * NT * DH]\
                                .rearrange("p (t d) -> p t d", t=NT)
                            scl = scales[:, 2 * kind + cs, bass.ds(l, 1), :] if not isinstance(s, int) else \
                                scales[:, 2 * kind + cs, l:l + 1, :]
                            dve.tensor_tensor(table[:, kind, cs, :, :], base, scl.to_broadcast([P, NT, DH]),
                                              ALU.mult).then_inc(tab_done, 1)
                for v in range(SLOTS):
                    g = s * SLOTS + v
                    u, vv, st, pr = unit(s, par, v, L_V + 1)
                    if live(u, UNITS):
                        wait(dve, v_ready, u + 1)
                        if vv == 0:
                            wait(dve, o_ready, (st - 1) * SLOTS)
                        dve.tensor_copy(V[0:KW, pr, vv // 2, 512 * (vv % 2):512 * (vv % 2 + 1)],
                                        VT_ps[0:KW, :]).then_inc(v_evac, 1)
                    f, pr = batch(s, par, v, F_GEL)
                    if f is not None:
                        hidden(f, pr, [0, 1])
                    f, pr = batch(s, par, v, F_END)
                    if f is not None:
                        finish(f, pr)
                    f, pr = batch(s, par, v, F_BC)
                    if f is not None:
                        rstd = rn[:, LN_HALF, NORMS:].unsqueeze(2).to_broadcast([P, NT, P])
                        wait(dve, nw_seq, newton_count(*ln_newton(s, v)))
                        dve.tensor_tensor(diag[:, :, :], ident.unsqueeze(1).to_broadcast([P, NT, P]), rstd,
                                          ALU.mult).then_inc(diag_done, 1)
                    f, pr = batch(s, par, v, F_MID)
                    if f is not None:
                        b = f % B
                        xb = xT[:, b, :] if isinstance(f, int) else \
                            xT[:, bass.ds(b, 1), :].rearrange("p o n -> p (o n)")
                        wait(dve, wo_ready, f + 1)
                        dve.tensor_tensor(xm[:, pr, :], BANK_WO[:, 0:N], xb, ALU.add)\
                           .then_inc(mid_done, 1)
                    a, hp, st, pr = unit(s, par, v, L_RS)
                    if live(a, UNITS):
                        wait(dve, exp_done, (a + 1) * QB)
                        wait(dve, p_norm, a - 3)
                        dve.reciprocal(rs[:, hp % 4, :], sm[:, hp % 4, :]).then_inc(rs_done, 1)
                    if live(g, UNITS):
                        half, tile, kind = v // 4, (v // 2) % 2, v % 2
                        if v == 0 and par == 0:
                            wait(dve, tab_done, 4 * (s // 2 + 1))
                        q8 = QK_ps[:, :].rearrange("p (h c d) -> p h c d", h=8, c=2)
                        tab = table[:, kind, :, tile, :].rearrange("p a (c d) -> p a c d", c=2)
                        wait(dve, sq_done, g + 1)
                        wait(dve, tr_ready, g - 7)
                        dve.tensor_tensor(t1[:, v, :].rearrange("p (h d) -> p h d", h=8),
                                          QK_ps[:, :].rearrange("p (h d) -> p h d", h=8),
                                          table[:, kind, 0, tile, :].unsqueeze(1).to_broadcast([P, 8, DH]),
                                          ALU.mult).then_inc(t12_done, 1)
                        wait(dve, add_done, g - 1)
                        dve.tensor_tensor(t2[:, v % 2, :].rearrange("p (h c d) -> p h c d", h=8, c=2),
                                          q8[:, :, ::-1, :],
                                          tab[:, 1].unsqueeze(1).to_broadcast([P, 8, 2, DH // 2]),
                                          ALU.mult).then_inc(t12_done, 1)
                        dve.tensor_reduce(ss[:, half, 8 * (v % 4):8 * (v % 4 + 1)],
                                          sq[:, v % 2, :].rearrange("p (h d) -> p h d", h=8), AX_X, ALU.add)\
                           .then_inc(ss_done, 1)
                    a, hp, st, pr = unit(s, par, v, L_S)
                    if live(a, UNITS):
                        wait(dve, s_ready, a + 1)
                        wait(dve, exp_done, QB * (a - 1))
                        Sv = S_ps[hp % 2][:, 0:QB * KW].rearrange("p (m k) -> p m k", m=QB)
                        dve.tensor_reduce(nmx[:, hp % 2, :], Sv, AX_X, ALU.max, negate=True).then_inc(max_done, 1)
                    f, pr = batch(s, par, v, F_VCOPY)
                    if f is not None:
                        wait(dve, var_ready, f + 1)
                        dve.tensor_scalar(ss[:, LN_HALF, NORMS:], BANK_VAR[:, 0:NT], 1e-5, None, ALU.add)\
                           .then_inc(var_copied, 1)
                    if v % 4 == 3 and (live(g, UNITS) or f is not None):
                        half = v // 4
                        seq = newton_count(s, half) - NW_OPS
                        cols = NORMS + NT if half == LN_HALF else NORMS
                        x_, y_, t_ = ss[:, half, 0:cols], rn[:, half, 0:cols], nwt[:, 0:cols]
                        wait(dve, ss_done, upto(g + 1, UNITS))
                        if f is not None:
                            wait(dve, var_copied, f + 1)
                        dve.tensor_scalar(x_, x_, 1e-24, None, ALU.max).then_inc(nw_seq, 1)
                        wait(dve, nw_seq, seq + 1)
                        wait(dve, qk_norm, upto(g - 7, UNITS))
                        dve.tensor_scalar(y_.bitcast(I32), x_.bitcast(I32), -0.5, RSQRT_SEED,
                                          ALU.mult, ALU.add).then_inc(nw_seq, 1)
                        for n, (factor, const) in enumerate(NEWTON):
                            wait(dve, nw_seq, seq + 3 * n + 2)
                            dve.scalar_tensor_tensor(out=t_, in0=y_, scalar=factor, in1=y_, op0=ALU.mult,
                                                     op1=ALU.mult).then_inc(nw_seq, 1)
                            wait(dve, nw_seq, seq + 3 * n + 3)
                            dve.tensor_tensor(t_, t_, x_, ALU.mult).then_inc(nw_seq, 1)
                            wait(dve, nw_seq, seq + 3 * n + 4)
                            dve.scalar_tensor_tensor(out=y_, in0=t_, scalar=const, in1=y_, op0=ALU.subtract,
                                                     op1=ALU.mult).then_inc(nw_seq, 1)
                    f, pr = batch(s, par, v, F_CENT)
                    if f is not None:
                        wait(dve, mean_ready, f + 1)
                        wait(dve, xs_done, 2 * (f + 1))
                        dve.tensor_tensor(xc[:, :], xs[:, :], BANK_MEAN[:, 0:N], ALU.subtract)\
                           .then_inc(cent_done, 1)
                    f, pr = batch(s, par, v, F_XN)
                    if f is not None:
                        wait(dve, bc_ready, f + 1)
                        dve.tensor_tensor(xr[:, :], xc[:, :], BANK_BC[:, 0:N], ALU.mult).then_inc(xr_done, 1)
                        if pr == 0:
                            wait(dve, in_ffn, (f // B + 1) * 48)
                        wait(dve, xr_done, f + 1)
                        dve.tensor_scalar(xn[:, :], xr[:, :], prm[:, R_G:R_G + 1], prm[:, R_B:R_B + 1],
                                          ALU.mult, ALU.add).then_inc(xn_done, 1)
                    f, pr = batch(s, par, v, F_GEL)
                    if f is not None:
                        hidden(f, pr, [2])

            def hidden(f, par, chunks):
                for r_ in chunks:
                    w = FCH[r_][1]
                    wait(dve, gel_done, f * NCH + r_ + 1)
                    dve.scalar_tensor_tensor(out=hid[0:w, r_, :], in0=BANK_W1[r_][0:w, 0:N],
                                             scalar=prm[0:w, R_B1A + r_:R_B1A + r_ + 1], in1=gel[0:w, r_, :],
                                             op0=ALU.add, op1=ALU.mult).then_inc(hid_done, 1)

            def finish(f, par):
                b = f % B
                xb = xT[:, b, :] if isinstance(f, int) else xT[:, bass.ds(b, 1), :].rearrange("p o n -> p (o n)")
                wait(dve, w2_ready, f + 1)
                wait(dve, mid_done, f + 1)
                dve.scalar_tensor_tensor(out=xb, in0=BANK_W2[:, 0:N], scalar=prm[:, R_B2:R_B2 + 1],
                                         in1=xm[:, par, :], op0=ALU.add, op1=ALU.add).then_inc(ff_final, 1)

            all_steps(dve, step)
            for c in range(4):
                dve.wait_ge(g_done, c + 1)
                yc = yT[:, 2 * c:2 * c + 2, :]
                dve.tensor_tensor(yc, yc, xT[:, 2 * c:2 * c + 2, :], ALU.mult).then_inc(prod_done, 1)
            dve.wait_ge(in_x2, 16)
            for c in range(4):
                dve.wait_ge(oT_ready, c + 1)
                dve.tensor_tensor(o_tok[:, 4 * c:4 * c + 4, :], banks[c][:, :].rearrange("p (t d) -> p t d", t=4),
                                  x_tok[:, 4 * c:4 * c + 4, :], ALU.add).then_inc(o_done, 1)

        @block.gpsimd
        def _(pool):
            pool.memset(QT[:, :, :, :, :, :].rearrange("p a b c d e -> p (a b c d e)"), 0.0).then_inc(set_pool, 1)
            pool.memset(KT[:, :, :, 0:PAD], 0.0).then_inc(set_pool, 1)
            pool.memset(xw[:, :, 0:PAD + 1], 0.0).then_inc(set_pool, 1)
            pool.memset(hid[:, NCH - 1, :], 0.0).then_inc(set_pool, 1)
            pool.memset(xs[:, 0:1], 0.0).then_inc(set_pool, 1)
            pool.wait_ge(set_pool, 5)

            def step(s, par):
                for v in range(SLOTS):
                    g = s * SLOTS + v
                    u, vv, st, pr = unit(s, par, v, L_SCALE)
                    if live(u, UNITS):
                        if vv % 4 == 0:
                            wait(pool, nw_seq, newton_count(st, vv // 4))
                        wait(pool, add_done, u + 1)
                        w = t1[:, vv, :].rearrange("p (h d) -> p h d", h=8)
                        pool.tensor_tensor(w, w, rn[:, vv // 4, 8 * (vv % 4):8 * (vv % 4 + 1)].unsqueeze(2).to_broadcast([P, 8, DH]),
                                           ALU.mult).then_inc(qk_norm, 1)
                    a, hp, st, pr = unit(s, par, v, L_NORM)
                    if live(a, UNITS):
                        wait(pool, rs_done, a + 1)
                        pool.tensor_tensor(E[:, hp % 4, :, :], E[:, hp % 4, :, :],
                                           rs[:, hp % 4, :].unsqueeze(2).to_broadcast([P, QB, KW]),
                                           ALU.mult).then_inc(p_norm, 1)

                    if live(g, UNITS):
                        wait(pool, t12_done, 2 * (g + 1))
                        pool.tensor_tensor(t1[:, v, :], t1[:, v, :], t2[:, v % 2, :], ALU.add).then_inc(add_done, 1)
            all_steps(pool, step)


def shape_constants():
    c = np.zeros((P, C_ALL), np.float32)
    c[:, C_ID:C_ID + P] = np.eye(P, dtype=np.float32)
    q = np.arange(P)[:, None] % 64
    k = np.arange(KW)[None, :]
    allowed = (k >= q) & (k <= q + WINDOW)
    for m in range(QB):
        ok = allowed & (k >= WINDOW) if m == 0 else allowed
        c[:, C_MASK + KW * m:C_MASK + KW * (m + 1)] = np.where(ok, 0.0, -1e30)
    half = np.arange(0, DH, 2, dtype=np.float32)
    inv_freq = (1.0 / np.float32(10000.0) ** (half / DH)).astype(np.float32)
    t = np.arange(N, dtype=np.float32)
    freqs = t[:, None] * inv_freq[None, :]
    freqs = np.concatenate([freqs, freqs], -1)
    base = (half + np.float32(0.4 * DH)) / np.float32(1.4 * DH)
    power = (t - N // 2) / (WINDOW // 2)
    scale = (base[None, :] ** power[:, None]).astype(np.float32)
    scale = np.concatenate([scale, scale], -1)
    sign = np.where(np.arange(DH) < DH // 2, -1.0, 1.0).astype(np.float32)
    cos, sin = np.cos(freqs), np.sin(freqs) * sign
    for i, tab in enumerate((QK_SCALE * cos * scale, QK_SCALE * sin * scale, cos / scale, sin / scale)):
        c[:, C_TAB + i * NT * DH:C_TAB + (i + 1) * NT * DH] = \
            tab.reshape(NT, P, DH).transpose(1, 0, 2).reshape(P, NT * DH).astype(np.float32)
    return c


def kernel(**inputs):
    import concourse.bacc as bacc
    from concourse.bass_utils import run_bass_kernel_spmd

    i = {k: np.asarray(v) for k, v in inputs.items()}

    def cols(a, n):
        a = np.concatenate([a, np.zeros((DEPTH, n * P - a.shape[1]), a.dtype)], 1)
        return a.reshape(DEPTH, n, P).transpose(0, 2, 1)

    qs, ks = i["L0_ffn_q_scale"], i["L0_ffn_k_scale"]
    swap = np.concatenate([np.arange(DH // 2, DH), np.arange(DH // 2)])
    w2 = i["L0_ffn_W2"]
    w2 = np.concatenate([w2, np.zeros((DEPTH, NCH * P - FF, D), w2.dtype)], 1)
    b1 = i["L0_ffn_b1"]
    arrays = {
        "x": i["L0_attn_x"],
        "rec_w": np.stack([i["L0_attn_W_u"].T, i["L0_attn_W_g"].T, i["L0_attn_A"], i["L0_attn_A"].T,
                           i["L0_attn_Bm"].T, i["L0_attn_Cm"].T], 1),
        "rec_b": np.stack([i["L0_attn_b_u"], i["L0_attn_b_g"], i["L0_attn_D"]], 1),
        "wqkv": i["L0_ffn_Wqkv"],
        "wo": i["L0_ffn_Wo"].reshape(DEPTH, HP, P, D).transpose(0, 2, 1, 3),
        "w1": i["L0_ffn_W1"],
        "w2": w2.reshape(DEPTH, NCH, P, D).transpose(0, 2, 1, 3),
        "params": np.concatenate([cols(i["L0_ffn_ln_g"], 1), cols(i["L0_ffn_ln_b"], 1), cols(b1[:, :FF], NCH),
                                  cols(b1[:, FF:], NCH), cols(i["L0_ffn_b2"], 1)], 2),
        "qk_scales": np.broadcast_to(np.stack([qs, qs[:, swap], ks, ks[:, swap]])[None], (P, 4, DEPTH, DH)),
        "consts": shape_constants(),
    }
    arrays = {k: np.ascontiguousarray(v) for k, v in arrays.items()}
    nc = bacc.Bacc("TRN2", target_bir_lowering=False, num_devices=1)
    aps = {k: nc.dram_tensor(f"in_{k}", v.shape, mybir.dt.from_np(v.dtype), kind="ExternalInput").ap()
           for k, v in arrays.items()}
    out = nc.dram_tensor("out", i["L0_attn_x"].shape, F32, kind="ExternalOutput").ap()
    gated_mix_kernel(nc, aps["x"], aps["rec_w"], aps["rec_b"], aps["wqkv"], aps["wo"], aps["w1"], aps["w2"],
                     aps["params"], aps["qk_scales"], aps["consts"], out)
    r = run_bass_kernel_spmd(nc, [{f"in_{k}": v for k, v in arrays.items()}], core_ids=[0])
    return r.results[0]["out"]
```

```python
from contextlib import ExitStack

import numpy as np

import concourse.bass as bass
from concourse import mybir

F32 = mybir.dt.float32
F32R = mybir.dt.float32r
BF16 = mybir.dt.bfloat16
I32 = mybir.dt.int32
ALU = mybir.AluOpType
ACT = mybir.ActivationFunctionType
AX_X = mybir.AxisListType.X

P = 128
B, N, D = 8, 256, 128
DEPTH, HEADS, DH, WINDOW = 6, 16, 64, 32
INNER = HEADS * DH
FF = int(D * 4 * 2 / 3)
FCH = [(c * P, min(P, FF - c * P)) for c in range(-(-FF // P))]
NCH = len(FCH)
QK_SCALE = 8.0
STEPS = DEPTH * B
NORMS = 4 * 8
SLOTS = 8
UNITS = STEPS * SLOTS
HP = HEADS // 2
QB = N // 64
KW = 96
PAD = WINDOW
NT = N // P
T = B * N
TILES = T // P
LOG_N = N.bit_length() - 1
Y_SLOT = 12
L_SCALE, L_TR = 4, 5
L_S = L_TR + 4
L_EXP, L_RS, L_NORM, L_PT, L_PV = L_S + 1, L_S + 2, L_S + 2, L_S + 3, L_S + 4
L_V = L_PV - SLOTS
F_WO = L_PV + SLOTS + 1
F_MID, F_MEAN, F_CENT, F_VAR = (F_WO + i for i in (1, 2, 2, 3))
F_VCOPY = F_VAR + 1 + (SLOTS // 2 - 1 - (F_VAR + 1) % (SLOTS // 2))
F_BC, F_XN, F_W1, F_GEL, F_W2, F_END = (F_VCOPY + i for i in (1, 1, 2, 3, 4, 5))
LEAD = -(-F_END // SLOTS)
RSQRT_SEED = float(0x5F1FFFF9)
NEWTON = ((0.703952253, 0.703952253 * 2.38924456), (0.5, 1.5))
C_ID, C_MASK, C_TAB = 0, P, P + QB * KW
C_ALL = C_TAB + 4 * NT * DH
R_G, R_B, R_B1A, R_B1G, R_B2 = 0, 1, 2, 2 + NCH, 2 + 2 * NCH
R_ALL = 3 + 2 * NCH


def live(unit, count):
    return 0 <= unit < count if isinstance(unit, int) else True


def unit(s, par, v, lag):
    back = (v - lag) // SLOTS
    return s * SLOTS + v - lag, (v - lag) % SLOTS, s + back, (par + back) % 2


def batch(s, par, v, lag):
    back = (v - lag) // SLOTS
    here = (v - lag) % SLOTS == 0 and live(s + back, STEPS)
    return (s + back if here else None), (par + back) % 2


def v_units(s, v, lag):
    return upto(s * (SLOTS // 2) + (v - lag) // 2 + 1, STEPS * (SLOTS // 2))


def upto(count, most):
    return min(count, most) if isinstance(count, int) else count


def wait(eng, sem, count):
    if not isinstance(count, int) or count > 0:
        eng.wait_ge(sem, count)


def in_fill(s, v, end):
    return 2 * (s * SLOTS + v) + end if isinstance(s, int) else 10 ** 6


def scan_pieces():
    pieces = []
    ups = [(r, 2 ** (r + 1) - 1, N >> (r + 1)) for r in range(LOG_N)]
    downs = [(r, 3 * 2 ** r - 1, (N >> (r + 1)) - 1) for r in reversed(range(LOG_N - 1))]
    for r, first, count in ups + downs:
        nb = min(B, 512 // count)
        pieces += [(r, 2 ** r, first, count, b0, nb) for b0 in range(0, B, nb)]
    return pieces


def all_steps(eng, step):
    for s in range(LEAD):
        step(s, s % 2, s % B)
    with eng.Fori(0, DEPTH - 1) as l:
        for i in range(LEAD, LEAD + B):
            step(B * l + i, i % 2, i % B)
    with eng.Fori(((DEPTH - 1) * B + LEAD) // 2, STEPS // 2) as j:
        step(2 * j, 0, None)
        step(2 * j + 1, 1, None)
    for s in range(STEPS, STEPS + LEAD):
        step(s, s % 2, None)


def gated_mix_kernel(nc, x, rec_w, rec_b, wqkv, wo, w1, w2, params, qk_scales, consts, y_spill, out):
    with ExitStack() as ctx:
        def sb(name, shape, dt=F32):
            return ctx.enter_context(nc.sbuf_tensor(name, shape, dt))

        def sem(name):
            return ctx.enter_context(nc.semaphore(name))

        cst = sb("cst", [P, C_ALL])
        ident = cst[:, C_ID:C_ID + P]
        ident_bf = sb("ident_bf", [P, P], BF16)
        mask_bf = sb("mask_bf", [P, QB * KW], BF16)
        mean_w = sb("mean_w", [P, P])
        ones = sb("ones", [P, P])
        scales = sb("scales", [P, 4, DH])
        w_raw = sb("w_raw", [P, 512])
        w_hi = sb("w_hi", [P, 3 * INNER], F32R)
        w_lo = sb("w_lo", [P, 3 * INNER], F32R)
        wo_sb = sb("wo_sb", [P, HP, D])
        w1_sb = sb("w1_sb", [P, 2 * FF])
        w2_sb = sb("w2_sb", [P, NCH, D])
        prm = sb("prm", [P, R_ALL])
        xT = sb("xT", [P, B, N])
        x_hi = sb("x_hi", [P, 2, PAD + N], F32R)
        x_lo = sb("x_lo", [P, 2, PAD + N], F32R)
        table = sb("table", [P, 2, 2, NT, DH])
        sq = sb("sq", [P, 2, 512])
        t1 = sb("t1", [P, 8, 512])
        t2 = sb("t2", [P, 2, 512])
        ss = sb("ss", [P, 2, NORMS + NT])
        rn = sb("rn", [P, 2, NORMS + NT])
        nwt = sb("nwt", [P, NORMS + NT])
        QT = sb("QT", [P, 2, HP, QB, 2, 64])
        KT = sb("KT", [P, 2, HP, PAD + N])
        V = sb("V", [P, 2, QB, INNER])
        v_tok = sb("v_tok", [P, NT, INNER])
        nmx = sb("nmx", [P, 2, QB])
        sm = sb("sm", [P, 4, QB])
        rs = sb("rs", [P, 4, QB])
        E = sb("E", [P, 4, QB, KW])
        PT = sb("PT", [KW, 2, QB, P])
        OT = sb("OT", [P, 2, HP, N])
        xm = sb("xm", [P, 2, N])
        xs = sb("xs", [P, N])
        xc = sb("xc", [P, N])
        xq = sb("xq", [P, N])
        diag = xq[:, :].rearrange("p (t q) -> p t q", t=NT)
        hid = sb("hid", [P, NCH, N])
        x_tok = V[:, 0, 0:2, :].rearrange("p a b -> p (a b)").rearrange("p (t d) -> p t d", d=D)
        o_tok = V[:, 0, 2:4, :].rearrange("p a b -> p (a b)").rearrange("p (t d) -> p t d", d=D)
        U = V[:, 1, 0:2, :].rearrange("p a b -> p (a b)")
        yT = OT[:, 1, :, :]
        y_back = V[:, 1, 0:2, :].rearrange("p a b -> p (a b)").rearrange("p (b n) -> p b n", b=B)
        G = V[:, 1, 2:4, :].rearrange("p a b -> p (a b)")
        Z = U.rearrange("p (b n) -> p b n", b=B)
        rw = E[:, 0:2, :, :].rearrange("p a m k -> p (a m k)").rearrange("p (a n) -> p a n", n=P)
        rb = sb("rb", [P, 3])
        powers = OT[:, 1, :, :].rearrange("p a b -> p (a b)").rearrange("p (r a n) -> p r a n", a=2, n=P)
        stats = sb("stats", [P, TILES, 6])
        mv = sb("mv", [P, TILES, 2])
        rst = sb("rst", [P, TILES])
        eps = sb("eps", [P, 1])

        def bank(name):
            return ctx.enter_context(nc.psum_tensor(name, [P, 512], F32))

        S_ps = [bank("S0"), bank("S1")]
        PT_ps = bank("PTb")
        O_ps = bank("Ob")
        F_ps = [bank("F0"), bank("F1")]
        QK_ps = bank("QKb")
        VT_ps = bank("VTb")
        banks = [S_ps[0], S_ps[1], PT_ps, O_ps, F_ps[0], F_ps[1], QK_ps, VT_ps]

        in_x, in_rec, in_cst, in_scl = sem("in_x"), sem("in_rec"), sem("in_cst"), sem("in_scl")
        in_w, w_split, in_wo, in_ffn = sem("in_w"), sem("w_split"), sem("in_wo"), sem("in_ffn")
        set_pool, set_dve = sem("set_pool"), sem("set_dve")
        st_done, mv_done, sd_done, ln_done, lnT_ready, xT_done = (
            sem("st_done"), sem("mv_done"), sem("sd_done"), sem("ln_done"), sem("lnT_ready"), sem("xT_done"))
        rec_mm, rec_act, u_done, uB_ready, Z_done, pow_ready, pow_done, yT_done = (
            sem("rec_mm"), sem("rec_act"), sem("u_done"), sem("uB_ready"), sem("Z_done"), sem("pow_ready"),
            sem("pow_done"), sem("yT_done"))
        scan_ready = sem("scan_ready")
        x_staged, x_low, tab_done = sem("x_staged"), sem("x_low"), sem("tab_done")
        qk_ready, sq_done, t12_done, ss_done = sem("qk_ready"), sem("sq_done"), sem("t12_done"), sem("ss_done")
        add_done, nw_seq, qk_norm = sem("add_done"), sem("nw_seq"), sem("qk_norm")
        tr_ready, tr_evac, v_ready, v_evac = sem("tr_ready"), sem("tr_evac"), sem("v_ready"), sem("v_evac")
        v_moved, y_saved, in_y = sem("v_moved"), sem("y_saved"), sem("in_y")
        zeroed = sem("zeroed")
        s_ready, max_done, exp_done = sem("s_ready"), sem("max_done"), sem("exp_done")
        rs_done, p_norm = sem("rs_done"), sem("p_norm")
        pt_ready, pt_evac, o_ready, o_evac = sem("pt_ready"), sem("pt_evac"), sem("o_ready"), sem("o_evac")
        wo_ready, mean_ready, var_ready, bc_ready, w1_ready, w2_ready = (
            sem("wo_ready"), sem("mean_ready"), sem("var_ready"), sem("bc_ready"), sem("w1_ready"), sem("w2_ready"))
        mid_done, xs_done, cent_done, xq_done = (
            sem("mid_done"), sem("xs_done"), sem("cent_done"), sem("xq_done"))
        var_copied, diag_done, xr_done, xn_done, gel_done, hid_done, ff_final = (
            sem("var_copied"), sem("diag_done"), sem("xr_done"), sem("xn_done"), sem("gel_done"), sem("hid_done"),
            sem("ff_final"))
        g_done, prod_done, oT_ready, o_done, stored = (
            sem("g_done"), sem("prod_done"), sem("oT_ready"), sem("o_done"), sem("stored"))
        in_x2 = sem("in_x2")

        BANK_WO, BANK_W2, BANK_MEAN, BANK_VAR, BANK_BC = (F_ps[i] for i in (0, 1, 0, 1, 0))
        BANK_W1 = [F_ps[1], F_ps[0], F_ps[1]]
        NW_OPS = 2 + 3 * len(NEWTON)

        W_CHUNKS = ([(kind * INNER + 512 * half, 4 * half + 2 + kind) for half in range(2) for kind in range(2)]
                    + [(2 * INNER + 512 * half, 4 + 2 * half) for half in range(2)])
        NW = len(W_CHUNKS)

        def split_slot(c):
            return W_CHUNKS[c][1] + 1 + (L_V if c >= 4 else 0)

        V_MOVES = []
        for t in range(NT):
            for m in range(QB):
                first, last = max(64 * m - PAD, P * t), min(64 * m - PAD + KW, P * (t + 1))
                if first < last:
                    V_MOVES.append((t, first - P * t, last - first, m, first - (64 * m - PAD)))

        LN_HALF = (F_VCOPY % SLOTS) // 4

        def newton_count(s, half):
            if isinstance(s, int) and s >= STEPS:
                return (2 * STEPS + s - STEPS + 1) * NW_OPS
            return (2 * s + half + 1) * NW_OPS

        def ln_newton(s, v):
            return s + (v - 1) // SLOTS, LN_HALF

        SCAN = scan_pieces()

        def scan_z(piece, back):
            _, k, first, count, b0, nb = piece
            t0 = first - back
            return Z[:, b0:b0 + nb, t0:t0 + 2 * k * (count - 1) + 1:2 * k]

        def scan_bank(i, piece):
            count, nb = piece[3], piece[5]
            return banks[i % 4][:, 0:nb * count].rearrange("p (b n) -> p b n", b=nb)

        block = ctx.enter_context(nc.Block())

        @block.sync
        def _(sp):
            sp.dma_start(x_tok, x.rearrange("b (t p) d -> p (b t) d", p=P)).then_inc(in_x, 16)
            sp.dma_start(cst[:, :], consts).then_inc(in_cst, 16)
            sp.dma_start(rw[:, :, :], rec_w).then_inc(in_rec, 16)
            sp.dma_start(rb[:, :], rec_b).then_inc(in_rec, 16)
            sp.dma_start(scales[:, :, :], qk_scales[0]).then_inc(in_scl, 16)
            sp.dma_start(wo_sb[:, :, :], wo[0]).then_inc(in_wo, 16)
            sp.dma_start(w1_sb[:, :], w1[0]).then_inc(in_ffn, 16)
            sp.dma_start(w2_sb[:, :, :], w2[0]).then_inc(in_ffn, 16)
            sp.dma_start(prm[:, :], params[0]).then_inc(in_ffn, 16)
            for c, (col, _) in enumerate(W_CHUNKS):
                if c:
                    sp.wait_ge(w_split, 2 * c)
                sp.dma_start(w_raw[:, :], wqkv[0, :, col:col + 512]).then_inc(in_w, 16)
            def load_layer(s, v, b_):
                l = s // B if b_ < B - 1 else (s + 1) // B
                b_ = (b_ + 1) % B - 1
                slot = b_ * SLOTS + v + SLOTS
                for c, (col, _) in enumerate(W_CHUNKS):
                    if slot == (split_slot(c - 1) if c else 0):
                        wait(sp, w_split, (l * NW + c) * 2)
                        sp.dma_start(w_raw[:, :], wqkv[bass.ds(l, 1)].rearrange("o p n -> (o p) n")[:, col:col + 512])\
                          .then_inc(in_w, 16)
                if slot == 1:
                    wait(sp, tab_done, l * 4)
                    sp.dma_start(scales[:, :, :], qk_scales[bass.ds(l, 1)].rearrange("o p c d -> (o p) c d"))\
                      .then_inc(in_scl, 16)
                if slot == F_WO + 1:
                    wait(sp, wo_ready, l * B)
                    sp.dma_start(wo_sb[:, :, :], wo[bass.ds(l, 1)].rearrange("o p h n -> (o p) h n")).then_inc(in_wo, 16)
                if slot == F_END + 1:
                    wait(sp, ff_final, l * B)
                    sp.dma_start(w1_sb[:, :], w1[bass.ds(l, 1)].rearrange("o p n -> (o p) n")).then_inc(in_ffn, 16)
                    sp.dma_start(w2_sb[:, :, :], w2[bass.ds(l, 1)].rearrange("o p c n -> (o p) c n"))\
                      .then_inc(in_ffn, 16)
                    sp.dma_start(prm[:, :], params[bass.ds(l, 1)].rearrange("o p n -> (o p) n")).then_inc(in_ffn, 16)

            def step(s, par, b_):
                for v in range(SLOTS):
                    if b_ is not None and not isinstance(s, int):
                        load_layer(s, v, b_)
                    if isinstance(s, int) and s * SLOTS + v == Y_SLOT:
                        sp.wait_ge(yT_done, 4)
                        sp.dma_start(y_spill, yT).then_inc(y_saved, 16)
                    u, vv, st, pr = unit(s, par, v, L_V)
                    if live(u, UNITS) and vv in (2, 6):
                        if vv == 2:
                            wait(sp, o_ready, (st - 1) * SLOTS)
                            wait(sp, zeroed, st + 1 if isinstance(st, int) and st < 2 else 2)
                        wait(sp, v_evac, v_units(st, vv, 0))
                        for t, row, rows, m, p0 in V_MOVES:
                            if t == vv // 4:
                                sp.dma_start(V[p0:p0 + rows, pr, m, :], v_tok[row:row + rows, t, :]).then_inc(v_moved, 16)

            all_steps(sp, step)
            sp.wait_ge(o_ready, UNITS)
            sp.dma_start(x_tok, x.rearrange("b (t p) d -> p (b t) d", p=P)).then_inc(in_x2, 16)
            sp.wait_ge(y_saved, 16)
            sp.dma_start(y_back, y_spill).then_inc(in_y, 16)
            for c in range(4):
                sp.wait_ge(o_done, c + 1)
                sp.dma_start(out[2 * c:2 * c + 2].rearrange("b (t p) d -> p (b t) d", p=P),
                             o_tok[:, 4 * c:4 * c + 4, :]).then_inc(stored, 16)
            sp.wait_ge(stored, 64)

        @block.tensor
        def _(pe):
            pe.wait_ge(in_cst, 16)
            pe.wait_ge(in_rec, 32)
            for t in range(TILES):
                pe.wait_ge(ln_done, t + 1)
                mm = pe.transpose(banks[t // 4][:, (t % 4) * P:(t % 4 + 1) * P], x_tok[:, t, :], ident)
                if t % 4 == 3:
                    mm.then_inc(lnT_ready, 1)
            xf = xT[:, :, :].rearrange("p b n -> p (b n)")
            Zf = U
            def square(r, out_):
                if r > 1:
                    pe.wait_ge(pow_done, r - 1)
                at, a_ = (rw[:, 3, :], rw[:, 2, :]) if r == 1 else (powers[:, r - 1, 0, :], powers[:, r - 1, 1, :])
                pe.matmul(out_[:, 0:P], a_, at, start=True, stop=True)
                pe.matmul(out_[:, P:2 * P], at, a_, start=True, stop=True).then_inc(pow_ready, 1)

            for c in range(4):
                pe.wait_ge(xT_done, c + 1)
                if c == 3:
                    pe.wait_ge(pow_done, 3)
                for k in range(2):
                    pe.matmul(banks[4 * k + c][:, :], rw[:, k, :], xf[:, 512 * c:512 * (c + 1)],
                              start=True, stop=True).then_inc(rec_mm, 1)
                if c < 3:
                    square(c + 1, banks[7])
            for c in range(4):
                pe.wait_ge(u_done, c + 1)
                pe.matmul(banks[c][:, :], rw[:, 4, :], G[:, 512 * c:512 * (c + 1)],
                          start=True, stop=True).then_inc(uB_ready, 1)
                square(c + 4, banks[4 + c])
            pe.wait_ge(pow_done, LOG_N - 1)

            def recurrence(i):
                if i < len(SCAN):
                    r, b0 = SCAN[i][0], SCAN[i][4]
                    pe.wait_ge(Z_done, 4 + i - (b0 > 0))
                    pe.matmul(scan_bank(i, SCAN[i]), rw[:, 3, :] if r == 0 else powers[:, r, 0, :],
                              scan_z(SCAN[i], SCAN[i][1]), start=True, stop=True).then_inc(scan_ready, 1)
                elif i < len(SCAN) + 4:
                    c = i - len(SCAN)
                    pe.wait_ge(Z_done, 4 + len(SCAN))
                    if c > 1:
                        pe.wait_ge(yT_done, c - 1)
                    pe.matmul(F_ps[c % 2][:, :], rw[:, 5, :], Zf[:, 512 * c:512 * (c + 1)],
                              start=True, stop=True).then_inc(scan_ready, 1)

            pe.wait_ge(set_pool, 6)
            pe.wait_ge(set_dve, 6)

            def project(out_, pr, token, col):
                hi, lo = x_hi[:, pr, token:token + P], x_lo[:, pr, token:token + P]
                pe.matmul(out_[:, :], hi, w_hi[:, col:col + 512], start=True, stop=False)
                pe.matmul(out_[:, :], hi, w_lo[:, col:col + 512], start=False, stop=False)
                return pe.matmul(out_[:, :], lo, w_hi[:, col:col + 512], start=False, stop=True)

            def step(s, par, b_):
                for v in range(SLOTS):
                    g = s * SLOTS + v
                    recurrence(in_fill(s, v, 0))
                    if live(g, UNITS):
                        if v == 0:
                            wait(pe, x_staged, 2 * (s + 1))
                            wait(pe, x_low, 2 * (s + 1))
                        if b_ == 0 and v in (0, 1, 4, 5):
                            wait(pe, w_split, 2 * (s // B * NW + 1 + 2 * (v // 4) + v % 4))
                        wait(pe, t12_done, 2 * g)
                        half, tile, kind = v // 4, (v // 2) % 2, v % 2
                        project(QK_ps, par, PAD + P * tile, kind * INNER + 512 * half).then_inc(qk_ready, 1)
                    u, vv, st, pr = unit(s, par, v, L_TR)
                    if live(u, UNITS):
                        wait(pe, qk_norm, u + 1)
                        wait(pe, v_evac, v_units(s, v - 1, L_V))
                        wait(pe, tr_evac, 2 * u)
                        for i in range(4):
                            mm = pe.transpose(VT_ps[:, P * i:P * (i + 1)], t1[:, vv, P * i:P * (i + 1)], ident)
                        mm.then_inc(tr_ready, 1)
                    a, hp, st, pr = unit(s, par, v, L_S)
                    if live(a, UNITS):
                        if hp % 4 == 0:
                            wait(pe, tr_evac, 2 * (st * SLOTS + 4 * (hp // 4 + 1)))
                        wait(pe, exp_done, QB * (a - 1))
                        for m in range(QB):
                            pe.matmul(S_ps[hp % 2][:, KW * m:KW * (m + 1)],
                                      QT[:, pr, hp, m, :, :].rearrange("p h q -> p (h q)"),
                                      KT[:, pr, hp, 64 * m:64 * m + KW],
                                      start=(m == 0), stop=False, skip_group_check=True)
                        pe.matmul(S_ps[hp % 2][:, 0:QB * KW], ident_bf[:, :], mask_bf[:, :], start=False, stop=True,
                                  skip_group_check=True).then_inc(s_ready, 1)
                    f, pr = batch(s, par, v, F_MEAN)
                    if f is not None:
                        wait(pe, xs_done, 2 * (f + 1))
                        pe.matmul(BANK_MEAN[:, 0:N], mean_w[:, :], xs[:, :], start=True, stop=True)\
                          .then_inc(mean_ready, 1)
                    f, pr = batch(s, par, v, F_VAR)
                    if f is not None:
                        wait(pe, xq_done, f + 1)
                        wait(pe, ff_final, f)
                        for t in range(NT):
                            mm = pe.matmul(BANK_VAR[:, t:t + 1], xq[:, P * t:P * (t + 1)], mean_w[:, 0:1],
                                           start=True, stop=True)
                        mm.then_inc(var_ready, 1)
                    f, pr = batch(s, par, v, F_GEL)
                    if f is not None:
                        ff_w1(f, pr, [2])
                    a, hp, st, pr = unit(s, par, v, L_PT)
                    if live(a, UNITS):
                        wait(pe, p_norm, a + 1)
                        wait(pe, pt_evac, a)
                        for m in range(QB):
                            mm = pe.transpose(PT_ps[0:KW, P * m:P * (m + 1)], E[:, hp % 4, m, :], ident)
                        mm.then_inc(pt_ready, 1)
                    u, vv, st, pr = unit(s, par, v, L_V)
                    if live(u, UNITS) and vv % 2 == 0:
                        if vv < 4 and pr == 0:
                            wait(pe, w_split, 2 * (st // B * NW + NW - 1 + vv // 2))
                        if not live(g - L_TR, UNITS):
                            wait(pe, v_evac, v_units(st, vv, 0) - 1)
                        wait(pe, tr_evac, 2 * upto(g - L_TR + 1, UNITS))
                        tile, half = vv // 4, vv // 2 % 2
                        project(VT_ps, pr, PAD + P * tile, 2 * INNER + 512 * half).then_inc(v_ready, 1)
                    a, hp, st, pr = unit(s, par, v, L_PV)
                    if live(a, UNITS):
                        if hp == 0:
                            wait(pe, v_moved, (st + 1) * len(V_MOVES) * 16)
                        wait(pe, pt_evac, a + 1)
                        wait(pe, o_evac, a)
                        for m in range(QB):
                            for h in range(2):
                                mm = pe.matmul(O_ps[64 * h:64 * h + 64, 64 * m:64 * m + 64],
                                               V[0:KW, pr, m, (2 * hp + h) * DH:(2 * hp + h + 1) * DH],
                                               PT[:, hp % 2, m, 64 * h:64 * h + 64], start=True, stop=True)
                        mm.then_inc(o_ready, 1)
                    recurrence(in_fill(s, v, 1))
                    f, pr = batch(s, par, v, F_BC)
                    if f is not None:
                        wait(pe, diag_done, f + 1)
                        pe.matmul(BANK_BC[:, 0:N], ones[:, :], diag[:, :, :].rearrange("p t q -> p (t q)"),
                                  start=True, stop=True).then_inc(bc_ready, 1)
                    f, pr = batch(s, par, v, F_WO)
                    if f is not None:
                        if pr == 0:
                            wait(pe, in_wo, (f // B + 1) * 16)
                        wait(pe, hid_done, (f - 1) * NCH + 2)
                        wait(pe, o_evac, (f + 1) * SLOTS)
                        for h in range(HP):
                            mm = pe.matmul(BANK_WO[:, 0:N], wo_sb[:, h, :], OT[:, pr, h, :],
                                           start=(h == 0), stop=(h == HP - 1))
                        mm.then_inc(wo_ready, 1)
                    f, pr = batch(s, par, v, F_W1)
                    if f is not None:
                        if pr == 0:
                            wait(pe, in_ffn, (f // B + 1) * 48)
                        wait(pe, xn_done, f + 1)
                        ff_w1(f, pr, [0, 1])
                    f, pr = batch(s, par, v, F_W2)
                    if f is not None:
                        wait(pe, hid_done, (f + 1) * NCH)
                        for r_ in range(NCH):
                            mm = pe.matmul(BANK_W2[:, 0:N], w2_sb[:, r_, :], hid[:, r_, :],
                                           start=(r_ == 0), stop=(r_ == NCH - 1))
                        mm.then_inc(w2_ready, 1)

            def ff_w1(f, par, chunks):
                for r_ in chunks:
                    c0, w = FCH[r_]
                    fb = BANK_W1[r_]
                    if r_ == 2:
                        wait(pe, hid_done, f * NCH + 1)
                    pe.matmul(fb[0:w, 0:N], w1_sb[:, c0:c0 + w], xc[:, :], start=True, stop=True)
                    pe.matmul(fb[0:w, N:2 * N], w1_sb[:, FF + c0:FF + c0 + w], xc[:, :],
                              start=True, stop=True).then_inc(w1_ready, 1)

            all_steps(pe, step)
            for c in range(4):
                pe.wait_ge(prod_done, c + 1)
                for i in range(4):
                    mm = pe.transpose(banks[c][:, P * i:P * (i + 1)], y_back[:, 2 * c + i // 2, (i % 2) * P:(i % 2 + 1) * P],
                                      ident)
                mm.then_inc(oT_ready, 1)

        @block.scalar
        def _(act):
            act.wait_ge(set_dve, 6)
            act.wait_ge(mv_done, TILES)
            act.activation(rst[:, :], mv[:, :, 1], ACT.Sqrt, bias=eps[:, 0:1]).then_inc(sd_done, 1)
            xf = xT[:, :, :].rearrange("p b n -> p (b n)")
            for c in range(4):
                act.wait_ge(lnT_ready, c + 1)
                act.copy(xf[:, 512 * c:512 * (c + 1)], banks[c][:, :]).then_inc(xT_done, 1)
            act.wait_ge(in_rec, 32)
            for c in range(4):
                act.wait_ge(rec_mm, 2 * c + 1)
                act.activation(U[:, 512 * c:512 * (c + 1)], banks[c][:, :], ACT.Gelu,
                               bias=rb[:, 0:1]).then_inc(rec_act, 1)
            for c in range(4):
                act.wait_ge(rec_mm, 2 * c + 2)
                act.activation(G[:, 512 * c:512 * (c + 1)], banks[4 + c][:, :], ACT.Sigmoid,
                               bias=rb[:, 1:2]).then_inc(rec_act, 1)

            def stage(s, par):
                b = s % B
                src = xT[:, b, :] if isinstance(s, int) else xT[:, bass.ds(b, 1), :].rearrange("p o n -> p (o n)")
                act.copy(x_hi[0:64, par, PAD:PAD + N], src[0:64, :]).then_inc(x_staged, 1)
                act.copy(x_hi[64:P, par, PAD + 1:PAD + N], src[64:P, 0:N - 1]).then_inc(x_staged, 1)

            act.wait_ge(xT_done, 4)
            act.wait_ge(set_pool, 6)
            stage(0, 0)

            def step(s, par, b_):
                for v in range(SLOTS):
                    g = s * SLOTS + v
                    f, pr = batch(s, par, v, F_GEL)
                    if f is not None:
                        gelus(f, pr, [0, 1])
                    f, pr = batch(s, par, v, F_VAR)
                    if f is not None:
                        wait(act, cent_done, f + 1)
                        act.activation(xq[:, :], xc[:, :], ACT.Square).then_inc(xq_done, 1)
                    if live(g, UNITS):
                        wait(act, qk_ready, g + 1)
                        wait(act, ss_done, g - 1)
                        act.activation(sq[:, v % 2, :], QK_ps[:, :], ACT.Square).then_inc(sq_done, 1)
                    u, vv, st, pr = unit(s, par, v, L_TR)
                    if live(u, UNITS):
                        half, tile, kind = vv // 4, (vv // 2) % 2, vv % 2
                        wait(act, tr_ready, u + 1)
                        if vv % 4 == 0:
                            wait(act, s_ready, (st - 2) * SLOTS + 4 * (half + 1))
                        if kind == 0:
                            for h in range(2):
                                act.copy(QT[64 * h:64 * h + 64, pr, 4 * half:4 * half + 4, 2 * tile:2 * tile + 2, h, :],
                                         VT_ps[64 * h:64 * h + 64, :].rearrange("p (i m q) -> p i m q", i=4, m=2))\
                                   .then_inc(tr_evac, 1)
                        else:
                            act.copy(KT[:, pr, 4 * half:4 * half + 4, PAD + P * tile:PAD + P * (tile + 1)],
                                     VT_ps[:, :].rearrange("p (i q) -> p i q", i=4)).then_inc(tr_evac, 2)
                    f, pr = batch(s, par, v, F_GEL)
                    if f is not None:
                        gelus(f, pr, [2])
                    a, hp, st, pr = unit(s, par, v, L_EXP)
                    if live(a, UNITS):
                        wait(act, max_done, a + 1)
                        wait(act, pt_ready, a - 3)
                        if isinstance(a, int) and a == 0:
                            wait(act, yT_done, 4)
                        for m in range(QB):
                            act.activation(E[:, hp % 4, m, :], S_ps[hp % 2][:, KW * m:KW * (m + 1)], ACT.Exp,
                                           bias=nmx[:, hp % 2, m:m + 1], accum_out=sm[:, hp % 4, m:m + 1])\
                               .then_inc(exp_done, 1)
                    a, hp, st, pr = unit(s, par, v, L_PT)
                    if live(a, UNITS):
                        wait(act, pt_ready, a + 1)
                        wait(act, o_ready, a - 1)
                        act.copy(PT[:, hp % 2, :, :], PT_ps[0:KW, :].rearrange("p (m q) -> p m q", m=QB))\
                           .then_inc(pt_evac, 1)
                    a, hp, st, pr = unit(s, par, v, L_PV)
                    if live(a, UNITS):
                        wait(act, o_ready, a + 1)
                        if isinstance(a, int) and a == SLOTS:
                            wait(act, y_saved, 16)
                        act.copy(OT[:, pr, hp, :], O_ps[:, 0:N]).then_inc(o_evac, 1)
                    f, pr = batch(s, par, v, F_MID)
                    if f is not None:
                        wait(act, mid_done, f + 1)
                        act.copy(xs[0:64, :], xm[0:64, pr, :]).then_inc(xs_done, 1)
                        act.copy(xs[64:P, 1:N], xm[64:P, pr, 0:N - 1]).then_inc(xs_done, 1)
                    if v == 5 and live(s + 1, STEPS):
                        wait(act, qk_ready, s * SLOTS)
                        wait(act, v_ready, s * (SLOTS // 2))
                        stage(s + 1, 1 - par)

            def gelus(f, par, chunks):
                for r_ in chunks:
                    w = FCH[r_][1]
                    wait(act, w1_ready, f * NCH + r_ + 1)
                    act.activation(hid[0:w, r_, :], BANK_W1[r_][0:w, N:2 * N], ACT.Gelu,
                                   bias=prm[0:w, R_B1G + r_:R_B1G + r_ + 1]).then_inc(gel_done, 1)

            all_steps(act, step)
            for c in range(4):
                act.wait_ge(ff_final, STEPS - 6 + 2 * c)
                act.activation(xT[:, 2 * c:2 * c + 2, :], xT[:, 2 * c:2 * c + 2, :], ACT.Silu).then_inc(g_done, 1)

        @block.vector
        def _(dve):
            dve.memset(eps[:, :], 1e-5).then_inc(set_dve, 1)
            dve.memset(mean_w[:, :], 1.0 / D).then_inc(set_dve, 1)
            dve.memset(ss[:, :, NORMS:], 1.0).then_inc(set_dve, 1)
            dve.memset(ones[:, :], 1.0).then_inc(set_dve, 1)
            dve.wait_ge(in_cst, 16)
            dve.tensor_copy(ident_bf[:, :], ident).then_inc(set_dve, 1)
            dve.tensor_copy(mask_bf[:, :], cst[:, C_MASK:C_MASK + QB * KW]).then_inc(set_dve, 1)
            dve.wait_ge(in_x, 16)
            for t in range(TILES):
                dve.bn_stats(stats[:, t, :], x_tok[:, t, :]).then_inc(st_done, 1)
            for t in range(TILES):
                dve.wait_ge(st_done, t + 1)
                dve.bn_aggr(mv[:, t, :], stats[:, t, :]).then_inc(mv_done, 1)
            dve.wait_ge(sd_done, 1)
            dve.reciprocal(rst[:, :], rst[:, :]).then_inc(sd_done, 1)
            dve.wait_ge(sd_done, 2)
            dve.wait_ge(mv_done, TILES)
            for t in range(TILES):
                dve.tensor_scalar(x_tok[:, t, :], x_tok[:, t, :], mv[:, t, 0:1], rst[:, t:t + 1],
                                  ALU.subtract, ALU.mult).then_inc(ln_done, 1)

            def keep_power(r, bank_):
                dve.wait_ge(pow_ready, r)
                dve.tensor_copy(powers[:, r, :, :].rearrange("p a n -> p (a n)"), bank_[:, 0:2 * P])\
                   .then_inc(pow_done, 1)

            for r in range(1, 4):
                keep_power(r, banks[7])
            for c in range(4):
                dve.wait_ge(rec_act, 4 + c + 1)
                dve.tensor_tensor(G[:, 512 * c:512 * (c + 1)], U[:, 512 * c:512 * (c + 1)],
                                  G[:, 512 * c:512 * (c + 1)], ALU.mult).then_inc(u_done, 1)
            for c in range(4):
                dve.wait_ge(uB_ready, c + 1)
                dve.wait_ge(u_done, 4)
                dve.tensor_copy(U[:, 512 * c:512 * (c + 1)], banks[c][:, :]).then_inc(Z_done, 1)
                keep_power(c + 4, banks[4 + c])

            def recurrence(i):
                if i < len(SCAN):
                    dve.wait_ge(scan_ready, i + 1)
                    dve.wait_ge(Z_done, 4 + i)
                    z = scan_z(SCAN[i], 0)
                    dve.tensor_tensor(z, z, scan_bank(i, SCAN[i]), ALU.add).then_inc(Z_done, 1)
                elif i < len(SCAN) + 4:
                    c = i - len(SCAN)
                    dve.wait_ge(scan_ready, i + 1)
                    dve.tensor_scalar(yT.rearrange("p b n -> p (b n)")[:, 512 * c:512 * (c + 1)], F_ps[c % 2][:, :],
                                      rb[:, 2:3], None, ALU.add).then_inc(yT_done, 1)

            def split_input(s, par):
                b = s % B
                src = xT[:, b, :] if isinstance(s, int) else xT[:, bass.ds(b, 1), :].rearrange("p o n -> p (o n)")
                wait(dve, x_staged, 2 * (s + 1))
                for p0, q0 in ((0, 0), (64, 1)):
                    cols = slice(PAD + q0, PAD + N)
                    dve.tensor_tensor(x_lo[p0:p0 + 64, par, cols], src[p0:p0 + 64, 0:N - q0],
                                       x_hi[p0:p0 + 64, par, cols].bitcast(F32), ALU.subtract).then_inc(x_low, 1)

            split_input(0, 0)

            def step(s, par, b_):
                if b_ == 0:
                    wait(dve, in_scl, (s // B + 1) * 16)
                    for kind in range(2):
                        for cs in range(2):
                            base = cst[:, C_TAB + (2 * kind + cs) * NT * DH:C_TAB + (2 * kind + cs + 1) * NT * DH]\
                                .rearrange("p (t d) -> p t d", t=NT)
                            scl = scales[:, 2 * kind + cs, :].unsqueeze(1)
                            dve.tensor_tensor(table[:, kind, cs, :, :], base, scl.to_broadcast([P, NT, DH]),
                                              ALU.mult).then_inc(tab_done, 1)
                for v in range(SLOTS):
                    g = s * SLOTS + v
                    recurrence(in_fill(s, v, 0))
                    if v == 6 and live(s + 1, STEPS):
                        split_input(s + 1, 1 - par)
                    f, pr = batch(s, par, v, F_GEL)
                    if f is not None:
                        hidden(f, pr, [0, 1])
                    f, pr = batch(s, par, v, F_END)
                    if f is not None:
                        finish(f, pr)
                    f, pr = batch(s, par, v, F_BC)
                    if f is not None:
                        rstd = rn[:, LN_HALF, NORMS:].unsqueeze(2).to_broadcast([P, NT, P])
                        wait(dve, nw_seq, newton_count(*ln_newton(s, v)))
                        dve.tensor_tensor(diag[:, :, :], ident.unsqueeze(1).to_broadcast([P, NT, P]), rstd,
                                          ALU.mult).then_inc(diag_done, 1)
                    f, pr = batch(s, par, v, F_MID)
                    if f is not None:
                        b = f % B
                        xb = xT[:, b, :] if isinstance(f, int) else \
                            xT[:, bass.ds(b, 1), :].rearrange("p o n -> p (o n)")
                        wait(dve, wo_ready, f + 1)
                        dve.tensor_tensor(xm[:, pr, :], BANK_WO[:, 0:N], xb, ALU.add)\
                           .then_inc(mid_done, 1)
                    a, hp, st, pr = unit(s, par, v, L_RS)
                    if live(a, UNITS):
                        wait(dve, exp_done, (a + 1) * QB)
                        wait(dve, p_norm, a - 3)
                        dve.reciprocal(rs[:, hp % 4, :], sm[:, hp % 4, :]).then_inc(rs_done, 1)
                    if live(g, UNITS):
                        half, tile, kind = v // 4, (v // 2) % 2, v % 2
                        if v == 0 and b_ == 0:
                            wait(dve, tab_done, 4 * (s // B + 1))
                        q8 = QK_ps[:, :].rearrange("p (h c d) -> p h c d", h=8, c=2)
                        tab = table[:, kind, :, tile, :].rearrange("p a (c d) -> p a c d", c=2)
                        wait(dve, sq_done, g + 1)
                        wait(dve, tr_ready, g - 7)
                        dve.tensor_tensor(t1[:, v, :].rearrange("p (h d) -> p h d", h=8),
                                          QK_ps[:, :].rearrange("p (h d) -> p h d", h=8),
                                          table[:, kind, 0, tile, :].unsqueeze(1).to_broadcast([P, 8, DH]),
                                          ALU.mult).then_inc(t12_done, 1)
                        wait(dve, add_done, g - 1)
                        dve.tensor_tensor(t2[:, v % 2, :].rearrange("p (h c d) -> p h c d", h=8, c=2),
                                          q8[:, :, ::-1, :],
                                          tab[:, 1].unsqueeze(1).to_broadcast([P, 8, 2, DH // 2]),
                                          ALU.mult).then_inc(t12_done, 1)
                        dve.tensor_reduce(ss[:, half, 8 * (v % 4):8 * (v % 4 + 1)],
                                          sq[:, v % 2, :].rearrange("p (h d) -> p h d", h=8), AX_X, ALU.add)\
                           .then_inc(ss_done, 1)
                    a, hp, st, pr = unit(s, par, v, L_S)
                    if live(a, UNITS):
                        wait(dve, s_ready, a + 1)
                        wait(dve, exp_done, QB * (a - 1))
                        Sv = S_ps[hp % 2][:, 0:QB * KW].rearrange("p (m k) -> p m k", m=QB)
                        dve.tensor_reduce(nmx[:, hp % 2, :], Sv, AX_X, ALU.max, negate=True).then_inc(max_done, 1)
                    u, vv, st, pr = unit(s, par, v, L_V)
                    if live(u, UNITS) and vv % 2 == 0:
                        wait(dve, v_ready, v_units(st, vv, 0))
                        if vv == 0:
                            wait(dve, v_moved, st * len(V_MOVES) * 16)
                        dve.tensor_copy(v_tok[:, vv // 4, 512 * (vv // 2 % 2):512 * (vv // 2 % 2 + 1)],
                                        VT_ps[:, :]).then_inc(v_evac, 1)
                    recurrence(in_fill(s, v, 1))
                    f, pr = batch(s, par, v, F_VCOPY)
                    if f is not None:
                        wait(dve, var_ready, f + 1)
                        dve.tensor_scalar(ss[:, LN_HALF, NORMS:], BANK_VAR[:, 0:NT], 1e-5, None, ALU.add)\
                           .then_inc(var_copied, 1)
                    if v % 4 == 3 and (live(g, UNITS) or f is not None):
                        half = v // 4
                        seq = newton_count(s, half) - NW_OPS
                        cols = NORMS + NT if half == LN_HALF else NORMS
                        x_, y_, t_ = ss[:, half, 0:cols], rn[:, half, 0:cols], nwt[:, 0:cols]
                        wait(dve, ss_done, upto(g + 1, UNITS))
                        if f is not None:
                            wait(dve, var_copied, f + 1)
                        dve.tensor_scalar(x_, x_, 1e-24, None, ALU.max).then_inc(nw_seq, 1)
                        wait(dve, nw_seq, seq + 1)
                        wait(dve, qk_norm, upto(g - 7, UNITS))
                        dve.tensor_scalar(y_.bitcast(I32), x_.bitcast(I32), -0.5, RSQRT_SEED,
                                          ALU.mult, ALU.add).then_inc(nw_seq, 1)
                        for n, (factor, const) in enumerate(NEWTON):
                            wait(dve, nw_seq, seq + 3 * n + 2)
                            dve.scalar_tensor_tensor(out=t_, in0=y_, scalar=factor, in1=y_, op0=ALU.mult,
                                                     op1=ALU.mult).then_inc(nw_seq, 1)
                            wait(dve, nw_seq, seq + 3 * n + 3)
                            dve.tensor_tensor(t_, t_, x_, ALU.mult).then_inc(nw_seq, 1)
                            wait(dve, nw_seq, seq + 3 * n + 4)
                            dve.scalar_tensor_tensor(out=y_, in0=t_, scalar=const, in1=y_, op0=ALU.subtract,
                                                     op1=ALU.mult).then_inc(nw_seq, 1)
                    f, pr = batch(s, par, v, F_CENT)
                    if f is not None:
                        wait(dve, mean_ready, f + 1)
                        wait(dve, xs_done, 2 * (f + 1))
                        dve.tensor_tensor(xc[:, :], xs[:, :], BANK_MEAN[:, 0:N], ALU.subtract)\
                           .then_inc(cent_done, 1)
                    f, pr = batch(s, par, v, F_XN)
                    if f is not None:
                        wait(dve, bc_ready, f + 1)
                        dve.tensor_tensor(xc[:, :], xc[:, :], BANK_BC[:, 0:N], ALU.mult).then_inc(xr_done, 1)
                        if pr == 0:
                            wait(dve, in_ffn, (f // B + 1) * 48)
                        wait(dve, xr_done, f + 1)
                        dve.tensor_scalar(xc[:, :], xc[:, :], prm[:, R_G:R_G + 1], prm[:, R_B:R_B + 1],
                                          ALU.mult, ALU.add).then_inc(xn_done, 1)
                    f, pr = batch(s, par, v, F_GEL)
                    if f is not None:
                        hidden(f, pr, [2])

            def hidden(f, par, chunks):
                for r_ in chunks:
                    w = FCH[r_][1]
                    wait(dve, gel_done, f * NCH + r_ + 1)
                    dve.scalar_tensor_tensor(out=hid[0:w, r_, :], in0=BANK_W1[r_][0:w, 0:N],
                                             scalar=prm[0:w, R_B1A + r_:R_B1A + r_ + 1], in1=hid[0:w, r_, :],
                                             op0=ALU.add, op1=ALU.mult).then_inc(hid_done, 1)

            def finish(f, par):
                b = f % B
                xb = xT[:, b, :] if isinstance(f, int) else xT[:, bass.ds(b, 1), :].rearrange("p o n -> p (o n)")
                wait(dve, w2_ready, f + 1)
                wait(dve, mid_done, f + 1)
                dve.scalar_tensor_tensor(out=xb, in0=BANK_W2[:, 0:N], scalar=prm[:, R_B2:R_B2 + 1],
                                         in1=xm[:, par, :], op0=ALU.add, op1=ALU.add).then_inc(ff_final, 1)

            all_steps(dve, step)
            dve.wait_ge(in_y, 16)
            for c in range(4):
                dve.wait_ge(g_done, c + 1)
                yc = y_back[:, 2 * c:2 * c + 2, :]
                dve.tensor_tensor(yc, yc, xT[:, 2 * c:2 * c + 2, :], ALU.mult).then_inc(prod_done, 1)
            dve.wait_ge(in_x2, 16)
            for c in range(4):
                dve.wait_ge(oT_ready, c + 1)
                dve.tensor_tensor(o_tok[:, 4 * c:4 * c + 4, :], banks[c][:, :].rearrange("p (t d) -> p t d", t=4),
                                  x_tok[:, 4 * c:4 * c + 4, :], ALU.add).then_inc(o_done, 1)

        @block.gpsimd
        def _(pool):
            pool.memset(QT[:, :, :, :, :, :].rearrange("p a b c d e -> p (a b c d e)"), 0.0).then_inc(set_pool, 1)
            pool.memset(KT[:, :, :, 0:PAD], 0.0).then_inc(set_pool, 1)
            for part in (x_hi, x_lo):
                pool.memset(part[:, :, 0:PAD + 1].bitcast(F32), 0.0).then_inc(set_pool, 1)
            pool.memset(hid[:, NCH - 1, :], 0.0).then_inc(set_pool, 1)
            pool.memset(xs[:, 0:1], 0.0).then_inc(set_pool, 1)
            pool.wait_ge(set_pool, 6)

            def zero_first_keys(pr):
                if pr == 0:
                    pool.wait_ge(lnT_ready, 4)
                else:
                    pool.wait_ge(yT_done, 4)
                pool.memset(V[0:PAD, pr, 0, :], 0.0).then_inc(zeroed, 1)

            def split_weights(l, c, in_use):
                col = W_CHUNKS[c][0]
                hi, lo, done = w_hi[:, col:col + 512], w_lo[:, col:col + 512], (l * NW + c) * 2
                if in_use is not None:
                    wait(pool, *in_use)
                wait(pool, in_w, (l * NW + c + 1) * 16)
                pool.tensor_tensor(hi, w_raw[:, :], ones[:, 0:1].to_broadcast([P, 512]), ALU.mult).then_inc(w_split, 1)
                wait(pool, w_split, done + 1)
                pool.tensor_tensor(lo, w_raw[:, :], hi.bitcast(F32), ALU.subtract).then_inc(w_split, 1)

            pool.wait_ge(set_dve, 6)
            for c in range(NW):
                split_weights(0, c, None)
            zero_first_keys(0)

            def step(s, par, b_):
                for v in range(SLOTS):
                    g = s * SLOTS + v
                    if isinstance(s, int) and g == Y_SLOT:
                        zero_first_keys(1)
                    if b_ in (0, B - 1) and not isinstance(s, int):
                        for c, (_, last) in enumerate(W_CHUNKS):
                            at = split_slot(c)
                            if (b_ == 0) == (at >= SLOTS) and at % SLOTS == v:
                                first = s - 1 if b_ == 0 else s
                                split_weights((first + 1) // B, c,
                                              (v_ready, v_units(first, last, 0)) if c >= 4 else
                                              (qk_ready, first * SLOTS + last + 1))
                    u, vv, st, pr = unit(s, par, v, L_SCALE)
                    if live(u, UNITS):
                        if vv % 4 == 0:
                            wait(pool, nw_seq, newton_count(st, vv // 4))
                        wait(pool, add_done, u + 1)
                        w = t1[:, vv, :].rearrange("p (h d) -> p h d", h=8)
                        pool.tensor_tensor(w, w, rn[:, vv // 4, 8 * (vv % 4):8 * (vv % 4 + 1)].unsqueeze(2).to_broadcast([P, 8, DH]),
                                           ALU.mult).then_inc(qk_norm, 1)
                    a, hp, st, pr = unit(s, par, v, L_NORM)
                    if live(a, UNITS):
                        wait(pool, rs_done, a + 1)
                        pool.tensor_tensor(E[:, hp % 4, :, :], E[:, hp % 4, :, :],
                                           rs[:, hp % 4, :].unsqueeze(2).to_broadcast([P, QB, KW]),
                                           ALU.mult).then_inc(p_norm, 1)
                    if live(g, UNITS):
                        wait(pool, t12_done, 2 * (g + 1))
                        pool.tensor_tensor(t1[:, v, :], t1[:, v, :], t2[:, v % 2, :], ALU.add).then_inc(add_done, 1)
            all_steps(pool, step)


def shape_constants():
    c = np.zeros((P, C_ALL), np.float32)
    c[:, C_ID:C_ID + P] = np.eye(P, dtype=np.float32)
    q = np.arange(P)[:, None] % 64
    k = np.arange(KW)[None, :]
    allowed = (k >= q) & (k <= q + WINDOW)
    for m in range(QB):
        ok = allowed & (k >= WINDOW) if m == 0 else allowed
        c[:, C_MASK + KW * m:C_MASK + KW * (m + 1)] = np.where(ok, 0.0, -1e30)
    half = np.arange(0, DH, 2, dtype=np.float32)
    inv_freq = (1.0 / np.float32(10000.0) ** (half / DH)).astype(np.float32)
    t = np.arange(N, dtype=np.float32)
    freqs = t[:, None] * inv_freq[None, :]
    freqs = np.concatenate([freqs, freqs], -1)
    base = (half + np.float32(0.4 * DH)) / np.float32(1.4 * DH)
    power = (t - N // 2) / (WINDOW // 2)
    scale = (base[None, :] ** power[:, None]).astype(np.float32)
    scale = np.concatenate([scale, scale], -1)
    sign = np.where(np.arange(DH) < DH // 2, -1.0, 1.0).astype(np.float32)
    cos, sin = np.cos(freqs), np.sin(freqs) * sign
    for i, tab in enumerate((QK_SCALE * cos * scale, QK_SCALE * sin * scale, cos / scale, sin / scale)):
        c[:, C_TAB + i * NT * DH:C_TAB + (i + 1) * NT * DH] = \
            tab.reshape(NT, P, DH).transpose(1, 0, 2).reshape(P, NT * DH).astype(np.float32)
    return c


def kernel(**inputs):
    import concourse.bacc as bacc
    from concourse.bass_utils import run_bass_kernel_spmd

    i = {k: np.asarray(v) for k, v in inputs.items()}

    def cols(a, n):
        a = np.concatenate([a, np.zeros((DEPTH, n * P - a.shape[1]), a.dtype)], 1)
        return a.reshape(DEPTH, n, P).transpose(0, 2, 1)

    qs, ks = i["L0_ffn_q_scale"], i["L0_ffn_k_scale"]
    swap = np.concatenate([np.arange(DH // 2, DH), np.arange(DH // 2)])
    w2 = i["L0_ffn_W2"]
    w2 = np.concatenate([w2, np.zeros((DEPTH, NCH * P - FF, D), w2.dtype)], 1)
    b1 = i["L0_ffn_b1"]
    arrays = {
        "x": i["L0_attn_x"],
        "rec_w": np.stack([i["L0_attn_W_u"].T, i["L0_attn_W_g"].T, i["L0_attn_A"], i["L0_attn_A"].T,
                           i["L0_attn_Bm"].T, i["L0_attn_Cm"].T], 1),
        "rec_b": np.stack([i["L0_attn_b_u"], i["L0_attn_b_g"], i["L0_attn_D"]], 1),
        "wqkv": i["L0_ffn_Wqkv"],
        "wo": i["L0_ffn_Wo"].reshape(DEPTH, HP, P, D).transpose(0, 2, 1, 3),
        "w1": i["L0_ffn_W1"],
        "w2": w2.reshape(DEPTH, NCH, P, D).transpose(0, 2, 1, 3),
        "params": np.concatenate([cols(i["L0_ffn_ln_g"], 1), cols(i["L0_ffn_ln_b"], 1), cols(b1[:, :FF], NCH),
                                  cols(b1[:, FF:], NCH), cols(i["L0_ffn_b2"], 1)], 2),
        "qk_scales": np.broadcast_to(np.stack([qs, qs[:, swap], ks, ks[:, swap]], 1)[:, None], (DEPTH, P, 4, DH)),
        "consts": shape_constants(),
    }
    arrays = {k: np.ascontiguousarray(v) for k, v in arrays.items()}
    nc = bacc.Bacc("TRN2", target_bir_lowering=False, num_devices=1)
    aps = {k: nc.dram_tensor(f"in_{k}", v.shape, mybir.dt.from_np(v.dtype), kind="ExternalInput").ap()
           for k, v in arrays.items()}
    out = nc.dram_tensor("out", i["L0_attn_x"].shape, F32, kind="ExternalOutput").ap()
    y_spill = nc.dram_tensor("y_spill", (P, B, N), F32, kind="Internal").ap()
    gated_mix_kernel(nc, aps["x"], aps["rec_w"], aps["rec_b"], aps["wqkv"], aps["wo"], aps["w1"], aps["w2"],
                     aps["params"], aps["qk_scales"], aps["consts"], y_spill, out)
    r = run_bass_kernel_spmd(nc, [{f"in_{k}": v for k, v in arrays.items()}], core_ids=[0])
    return r.results[0]["out"]
```
